# Optimizing a Trainium2 kernel written in Bass

```python
import numpy as np
import jax
import jax.numpy as jnp

def _softmax(x, axis=-1):
    return jax.nn.softmax(x, axis=axis)

def _gelu(x):
    return jax.nn.gelu(x, approximate=True)

def _silu(x):
    return jax.nn.silu(x)

def _sigmoid(x):
    return jax.nn.sigmoid(x)

def _layernorm(x, axis=-1, eps=1e-05):
    m = jnp.mean(x, axis=axis, keepdims=True)
    v = jnp.var(x, axis=axis, keepdims=True)
    return (x - m) / jnp.sqrt(v + eps)

def _scatter_add(tgt, idx, src, axis=0):
    return tgt.at[idx].add(src)

def _segment_sum(src, seg, n):
    return jax.ops.segment_sum(src, seg, n)
kernel_name = 'mk_vit_tower_d1_tok_img1024_r4_2ecd1b'

def setup_inputs(seed: int=0):
    np.random.seed(seed)
    _w = jnp.asarray

    def _rec_inputs():
        import jax
        import jax.numpy as jnp
        _rk = jax.random.key(seed)
        x = -0.00016672 + 0.999947 * jax.random.normal(jax.random.fold_in(_rk, 1), (32, 96, 96, 3), jnp.float32)
        return x
    x = _rec_inputs()

    def _L0_tok_setup():
        import jax, jax.numpy as jnp
        import numpy as np
        P = 16
        E = 256

        def patchify(images, patch_size):
            B, H, W, C = images.shape
            hp, wp = (H // patch_size, W // patch_size)
            x = images.reshape(B, hp, patch_size, wp, patch_size, C)
            x = x.transpose(0, 1, 3, 2, 4, 5)
            return x.reshape(B, hp * wp, patch_size * patch_size * C)
        key = jax.random.key(seed)
        k_img, k_w, k_b, k_pos = jax.random.split(key, 4)
        B, H, W, C = (64, 96, 96, 3)
        patch_dim = P * P * C
        patch_count = H // P * (W // P)
        images = jax.random.normal(k_img, (B, H, W, C), dtype=jnp.float32)
        W_proj = jax.random.normal(k_w, (E, patch_dim), dtype=jnp.float32) * patch_dim ** (-0.5)
        b_proj = jax.random.normal(k_b, (E,), dtype=jnp.float32) * 0.02
        pos_emb = jax.random.normal(k_pos, (patch_count, E), dtype=jnp.float32) * 0.02
        return {'images': images, 'W_proj': W_proj, 'b_proj': b_proj, 'pos_emb': pos_emb}
    _L0_tok_all = _L0_tok_setup()
    _L0_tok_in = {k: v for k, v in _L0_tok_all.items() if k in ('W_proj', 'b_proj', 'pos_emb')}
    del _L0_tok_all

    def _L0_attn_setup():
        import jax, jax.numpy as jnp
        import numpy as np
        HEADS = 16
        EPS = 1e-06
        key = jax.random.key(seed)
        k0, k1, k2, k3, k4 = jax.random.split(key, 5)
        b, t, dim = (2, 512, 256)
        scale = 0.02
        return {'hidden_states': jax.random.normal(k0, (b, t, dim), dtype=jnp.float32), 'Wq': jax.random.normal(k1, (dim, dim), dtype=jnp.float32) * scale, 'Wk': jax.random.normal(k2, (dim, dim), dtype=jnp.float32) * scale, 'Wv': jax.random.normal(k3, (dim, dim), dtype=jnp.float32) * scale, 'Wo': jax.random.normal(k4, (dim, dim), dtype=jnp.float32) * scale}
    _L0_attn_all = _L0_attn_setup()
    _L0_attn_in = {k: v for k, v in _L0_attn_all.items() if k in ('Wq', 'Wk', 'Wv', 'Wo')}
    del _L0_attn_all

    def _L0_ffn_setup():
        import jax, jax.numpy as jnp
        import numpy as np
        DIM = 256
        HIDDEN = 1024
        E = 8
        K = 2

        def _ffn_hidden(h, multiple_of=64):
            h = int(2 * h / 3)
            return multiple_of * ((h + multiple_of - 1) // multiple_of)
        EXP_HID = _ffn_hidden(HIDDEN)
        SH_HID = _ffn_hidden(HIDDEN // 2)

        def _swiglu(t, a, b, c):
            return jax.nn.silu(t @ a) * (t @ c) @ b
        key = jax.random.key(seed)
        ks = jax.random.split(key, 8)

        def xavier(k, shape, fan_in, fan_out):
            lim = np.sqrt(6.0 / (fan_in + fan_out)).astype(np.float32)
            return jax.random.uniform(k, shape, jnp.float32, -lim, lim)
        return {'x': jax.random.normal(ks[0], (2, 512, DIM), jnp.float32), 'gate_w': xavier(ks[1], (E, DIM), DIM, E), 'w1': xavier(ks[2], (E, DIM, EXP_HID), DIM, EXP_HID), 'w2': xavier(ks[3], (E, EXP_HID, DIM), EXP_HID, DIM), 'w3': xavier(ks[4], (E, DIM, EXP_HID), DIM, EXP_HID), 'sw1': xavier(ks[5], (DIM, SH_HID), DIM, SH_HID), 'sw2': xavier(ks[6], (SH_HID, DIM), SH_HID, DIM), 'sw3': xavier(ks[7], (DIM, SH_HID), DIM, SH_HID)}
    _L0_ffn_all = _L0_ffn_setup()
    _L0_ffn_in = {k: v for k, v in _L0_ffn_all.items() if k in ('gate_w', 'w1', 'w2', 'w3', 'sw1', 'sw2', 'sw3')}
    del _L0_ffn_all
    return {'x': x, 'L0_tok_W_proj': _L0_tok_in['W_proj'], 'L0_tok_b_proj': _L0_tok_in['b_proj'], 'L0_tok_pos_emb': _L0_tok_in['pos_emb'], 'L0_attn_Wq': _L0_attn_in['Wq'], 'L0_attn_Wk': _L0_attn_in['Wk'], 'L0_attn_Wv': _L0_attn_in['Wv'], 'L0_attn_Wo': _L0_attn_in['Wo'], 'L0_ffn_gate_w': _L0_ffn_in['gate_w'], 'L0_ffn_w1': _L0_ffn_in['w1'], 'L0_ffn_w2': _L0_ffn_in['w2'], 'L0_ffn_w3': _L0_ffn_in['w3'], 'L0_ffn_sw1': _L0_ffn_in['sw1'], 'L0_ffn_sw2': _L0_ffn_in['sw2'], 'L0_ffn_sw3': _L0_ffn_in['sw3']}

def reference(x, L0_tok_W_proj, L0_tok_b_proj, L0_tok_pos_emb, L0_attn_Wq, L0_attn_Wk, L0_attn_Wv, L0_attn_Wo, L0_ffn_gate_w, L0_ffn_w1, L0_ffn_w2, L0_ffn_w3, L0_ffn_sw1, L0_ffn_sw2, L0_ffn_sw3):
    import jax
    import jax.numpy as jnp

    def _L0_tok_ref(images, W_proj, b_proj, pos_emb):
        import jax, jax.numpy as jnp
        import numpy as np
        P = 16
        E = 256

        def patchify(images, patch_size):
            B, H, W, C = images.shape
            hp, wp = (H // patch_size, W // patch_size)
            x = images.reshape(B, hp, patch_size, wp, patch_size, C)
            x = x.transpose(0, 1, 3, 2, 4, 5)
            return x.reshape(B, hp * wp, patch_size * patch_size * C)
        patches = patchify(images, P)
        out = jnp.einsum('bnd,ed->bne', patches, W_proj) + b_proj + pos_emb[None, :, :]
        return out

    def _L0_attn_ref(hidden_states, Wq, Wk, Wv, Wo):
        import jax, jax.numpy as jnp
        import numpy as np
        HEADS = 16
        EPS = 1e-06
        b, t, dim = hidden_states.shape
        h = HEADS
        d = dim // h

        def proj(W):
            return (hidden_states @ W.T).reshape(b, t, h, d).transpose(0, 2, 1, 3)
        q = proj(Wq) * d ** (-0.5)
        k = proj(Wk)
        v = proj(Wv)
        s = jnp.einsum('bhqd,bhkd->bhqk', q, k)
        attn = 1.0 + s + 0.5 * s * s
        causal = jnp.tril(jnp.ones((t, t), dtype=bool))
        attn = jnp.where(causal, attn, 0.0)
        o = jnp.einsum('bhqk,bhkd->bhqd', attn, v)
        z = jnp.sum(attn, axis=-1, keepdims=True) + EPS
        o = o / z
        y = o.transpose(0, 2, 1, 3).reshape(b, t, dim)
        return y @ Wo.T

    def _L0_ffn_ref(x, gate_w, w1, w2, w3, sw1, sw2, sw3):
        import jax, jax.numpy as jnp
        import numpy as np
        DIM = 256
        HIDDEN = 1024
        E = 8
        K = 2

        def _ffn_hidden(h, multiple_of=64):
            h = int(2 * h / 3)
            return multiple_of * ((h + multiple_of - 1) // multiple_of)
        EXP_HID = _ffn_hidden(HIDDEN)
        SH_HID = _ffn_hidden(HIDDEN // 2)

        def _swiglu(t, a, b, c):
            return jax.nn.silu(t @ a) * (t @ c) @ b
        B, S, D = x.shape
        xt = x.reshape(-1, D)
        T = xt.shape[0]
        logits = xt @ gate_w.T
        scores = jax.nn.softmax(logits, axis=-1)
        topk_w, topk_i = jax.lax.top_k(scores, K)
        comb = jnp.zeros((T, E), x.dtype).at[jnp.arange(T)[:, None], topk_i].add(topk_w)
        y = jnp.zeros_like(xt)
        for e in range(E):
            y = y + comb[:, e:e + 1] * _swiglu(xt, w1[e], w2[e], w3[e])
        y = y.reshape(B, S, D)
        return y + _swiglu(x, sw1, sw2, sw3)
    h = _L0_tok_ref(x, L0_tok_W_proj, L0_tok_b_proj, L0_tok_pos_emb)
    h = h + _L0_attn_ref(_layernorm(h, axis=-1), L0_attn_Wq, L0_attn_Wk, L0_attn_Wv, L0_attn_Wo)
    h = h + _L0_ffn_ref(_layernorm(h, axis=-1), L0_ffn_gate_w, L0_ffn_w1, L0_ffn_w2, L0_ffn_w3, L0_ffn_sw1, L0_ffn_sw2, L0_ffn_sw3)
    return h

_drawn_inputs = setup_inputs


def setup_inputs(seed=0):
    import zlib

    import numpy as np

    out = dict(_drawn_inputs(seed))
    spreads = {}
    factors = {'L0_attn_Wq': 8.0, 'L0_attn_Wk': 8.0}
    for name, (base, spread) in spreads.items():
        noise = np.random.default_rng([zlib.crc32(name.encode()), seed]).standard_normal(out[name].shape)
        drawn = base * np.exp(spread * noise) if base else spread * noise
        out[name] = jnp.asarray(drawn.astype(out[name].dtype))
    for name, factor in factors.items():
        out[name] = (out[name] * factor).astype(out[name].dtype)
    return out
```

```python
from contextlib import ExitStack

import concourse.bass as bass
from concourse import mybir

F32 = mybir.dt.float32
I32 = mybir.dt.int32
U32 = mybir.dt.uint32
ALU = mybir.AluOpType
ACT = mybir.ActivationFunctionType
AX = mybir.AxisListType

P = 128
IMAGES, SIDE, CH, PATCH = 32, 96, 3, 16
PER_SIDE = SIDE // PATCH
SEQ = PER_SIDE * PER_SIDE
TOK = IMAGES * SEQ
D = 256
DC = D // P
PD = PATCH * PATCH * CH
PDC = PD // P
RUN = PATCH * CH
TILES = TOK // P
HEADS, HD = 16, 16
GIMG = 3
GT = GIMG * SEQ
GROUPS = -(-IMAGES // GIMG)
GPAD = GROUPS * GT
E, HID, SHID = 8, 704, 384
HALF = HID // 2
HC = -(-HID // P)
HLAST = HID - (HC - 1) * P
SHC = SHID // P
BLOCKS = (2 * TOK + E * (P - 1)) // P
SLOTS = BLOCKS * P
W1, W3, W2, WEXP = 0, DC * HID, 2 * DC * HID, 2 * DC * HID + HC * D
LN_EPS = 1e-5
ATT_EPS = 1e-6


def vit_moe(nc, x, w_proj, b_proj, pos_emb, wq, wk, wv, wo, gate_w, w1, w2, w3, sw1, sw2, sw3, out):
    ctx = ExitStack()
    with ctx:
        def sb(name, shape, dt=F32):
            return ctx.enter_context(nc.sbuf_tensor(name, shape, dt))

        def sem(name):
            return ctx.enter_context(nc.semaphore(name))

        slots_x = nc.dram_tensor("slots_x", [SLOTS, D], F32, kind="Internal").ap()
        slots_y = nc.dram_tensor("slots_y", [SLOTS, D], F32, kind="Internal").ap()

        experts = sb("experts", [P, E * WEXP])
        early = experts[:, 6 * WEXP:8 * WEXP]
        px = early[:, 0:3 * PD].rearrange("p (s d) -> p s d", s=3)
        probs = early[:, 0:2 * HEADS * GT].rearrange("p (a h q) -> p a h q", a=2, h=HEADS)
        o = 2 * HEADS * GT
        wproj_nat = early[:, o:o + DC * PD].rearrange("p (c d) -> p c d", c=DC)
        qk = early[:, o:o + 2 * 6 * GT].rearrange("p (a m q) -> p a m q", a=2, m=6)
        o += DC * PD
        w_nat = early[:, o:o + 4 * DC * D].rearrange("p (m c d) -> p m c d", m=4, c=DC)
        o += 4 * DC * D
        vaug = early[:, o:o + 2 * HEADS * (HD + 1)].rearrange("p (a h d) -> p a h d", a=2, h=HEADS)
        o += 2 * HEADS * (HD + 1)
        onorm = early[:, o:o + 2 * D].rearrange("p (a d) -> p a d", a=2)
        o += 2 * D
        xg = early[:, o:o + 2 * DC * GT].rearrange("p (a c q) -> p a c q", a=2, c=DC)
        shared_w = sb("shared_w", [P, 2 * DC * SHID + SHC * D])
        s1_sb = shared_w[:, 0:DC * SHID].rearrange("p (c n) -> p c n", c=DC)
        s3_sb = shared_w[:, DC * SHID:2 * DC * SHID].rearrange("p (c n) -> p c n", c=DC)
        s2_sb = shared_w[:, 2 * DC * SHID:].rearrange("p (c n) -> p c n", c=SHC)
        xa = sb("xa", [P, DC * GPAD])
        x1T = xa[:, :].rearrange("p (c t) -> p c t", c=DC)
        x2T = xa[:, 0:TILES * D].rearrange("p (t c q) -> p t c q", t=TILES, c=DC)
        hres = sb("hres", [P, TILES, D])
        xh2 = sb("xh2", [P, TILES, D])
        ob = sb("ob", [P, 3 * PD])
        pxT = ob[:, :].rearrange("p (s c q) -> p s c q", s=3, c=PDC)
        oT = ob[:, :].rearrange("p (c t w j) -> p c t w j", c=DC, t=TILES, w=2)
        fw = sb("fw", [P, PDC * D + 4 * DC * D])
        wprojT = fw[:, 0:PDC * D].rearrange("p (c n) -> p c n", c=PDC)
        wT = fw[:, PDC * D:].rearrange("p (m c n) -> p m c n", m=4, c=DC)
        o = 0
        xblk = fw[:, o:o + 2 * D].rearrange("p (a d) -> p a d", a=2); o += 2 * D
        xT = fw[:, o:o + D].rearrange("p (c q) -> p c q", c=DC); o += D
        gate = fw[:, o:o + HID]; o += HID
        hid = fw[:, o:o + HID]; o += HID
        hidT = fw[:, o:o + HC * P].rearrange("p (c q) -> p c q", c=HC); o += HC * P
        ysb = fw[:, o:o + 2 * D].rearrange("p (a d) -> p a d", a=2); o += 2 * D
        assert o <= PDC * D + 4 * DC * D
        xh1 = sb("xh1", [P, 3, D])
        yg = experts[:, 6 * WEXP:6 * WEXP + TILES * 2 * D].rearrange("p (t k d) -> p t k d", t=TILES, k=2)
        ident = sb("ident", [P, P])
        tri = sb("tri", [P, P])
        ones = sb("ones", [P, P])
        amask = sb("amask", [P, GT])
        gnat = sb("gnat", [E, D])
        gateT = sb("gateT", [P, DC, E])
        bias_b = sb("bias_b", [P, D])
        even = sb("even", [P, 1])
        odd = sb("odd", [P, 1])
        eps = sb("eps", [P, 1])
        one = sb("one", [P, 1])
        stats = sb("stats", [P, TILES, 6])
        mv = sb("mv", [P, TILES, 2])
        std = sb("std", [P, TILES])
        rstd = sb("rstd", [P, TILES])
        rz = sb("rz", [P, 2, HEADS])
        zz = sb("zz", [P, 2, HEADS])
        small = [0]

        def over(n):
            v = ob[:, small[0]:small[0] + n]
            small[0] += n
            assert small[0] <= 3 * PD
            return v

        def te(n=TILES):
            return over(n * E).rearrange("p (t e) -> p t e", e=E)
        rank = sb("rank", [P, TILES, E])
        thr = sb("thr", [P, E, TILES])
        bidx = sb("bidx", [P, BLOCKS, E])
        ldiff, ex, score, eq1, cand1, sel1, score2, eq2, cand2, sel2, sel = [te() for _ in range(11)]
        pos, ps1, ps2 = te(), te(), te()
        tsum = [te(8 + TILES), te(8 + TILES)]
        cmp_n = over(E * TILES).rearrange("p (e t) -> p e t", e=E)
        cmp_b = over(BLOCKS * E).rearrange("p (b e) -> p b e", e=E)
        csum = [over(8 + E), over(8 + E)]
        lmax, esum, rsum, best1, best2, w_1, w_2, slot1f, slot2f = [over(TILES) for _ in range(9)]
        blkf = over(BLOCKS)
        wts = sb("wts", [P, 2, TILES])
        slot = sb("slot", [P, 2, TILES], I32)
        blk = sb("blk", [P, BLOCKS], I32)

        bank = [ctx.enter_context(nc.psum_tensor(f"bank{i}", [P, 512], F32)) for i in range(8)]

        S = {}

        def s(name):
            if name not in S:
                S[name] = sem(name)
            return S[name]

        for n in ("wproj_in w_in gate_in bias_in pos_in px_in0 px_in1 px_in2 exp_in exp67_in shared_in zero_done "
                  "pool_step consts w_tr w_ev px_tr ev_a ev_b h_mm h_res st ag sd rs xh x_tr x_ev xg_c "
                  "qk_mm qk_ev v_mm v_ev s_mm sq a_rdy o_mm o_z o_r o_n oT_mm oT_ev "
                  "op_mm op_res st2 ag2 sd2 rs2 xh2_s x2_tr x2_ev lg_mm rt ex_s pre_mm sel_s slot_s blk_s "
                  "g_mm g_act g_mul g_tr g_ev y_mm y_add scat x_in0 x_in1 bx_tr bx_ev bg0 bg1 ba0 ba1 bm "
                  "bh_tr bh_ea bh_eb by_mm by_ev y_st0 y_st1 gat comb out_s pb_add").split():
            s(n)

        xv = x.rearrange("b (hp ph) w c -> (b hp) ph (w c)", ph=PATCH).rearrange("(j g) ph q -> g j ph q", g=3)
        outv = out.rearrange("b s d -> (b s) d").rearrange("(j t w) d -> t w j d", t=TILES, w=2)

        block = ctx.enter_context(nc.Block())

        def load_patches(eng, G, W):
            for w in range(2):
                c = (2 * W + w) * RUN
                eng.dma_start(px[64 * w:64 * w + 64, W, :].rearrange("p (a r) -> p a r", a=PATCH),
                              xv[G, :, :, c:c + RUN]).then_inc(s(f"px_in{W}"), 16)

        def load_expert(eng, e, name):
            at = experts[:, e * WEXP:(e + 1) * WEXP]
            eng.dma_start(at[:, W1:W3].rearrange("p (c n) -> p c n", c=DC),
                          w1[e].rearrange("(c p) n -> p c n", p=P)).then_inc(s(name), 16)
            eng.dma_start(at[:, W3:W2].rearrange("p (c n) -> p c n", c=DC),
                          w3[e].rearrange("(c p) n -> p c n", p=P)).then_inc(s(name), 16)
            full = (HC - 1) * P
            eng.dma_start(at[:, W2:W2 + (HC - 1) * D].rearrange("p (c n) -> p c n", c=HC - 1),
                          w2[e, 0:full, :].rearrange("(c p) n -> p c n", p=P)).then_inc(s(name), 16)
            eng.dma_start(at[0:HLAST, W2 + (HC - 1) * D:WEXP], w2[e, full:HID, :]).then_inc(s(name), 16)

        @block.sync
        def _(sp):
            sp.dma_start(wproj_nat, w_proj.rearrange("(c p) d -> p c d", p=P)).then_inc(s("wproj_in"), 16)
            for W in range(3):
                load_patches(sp, 0, W)
            for m, w in enumerate((wq, wk, wv, wo)):
                sp.dma_start(w_nat[:, m], w.rearrange("(c p) d -> p c d", p=P)).then_inc(s("w_in"), 16)
            sp.dma_start(gnat[:, :], gate_w).then_inc(s("gate_in"), 16)
            for G in range(1, 3):
                for W in range(3):
                    sp.wait_ge(s("px_tr"), 3 * (G - 1) + W + 1)
                    load_patches(sp, G, W)
            sp.dma_start(s1_sb, sw1.rearrange("(c p) n -> p c n", p=P)).then_inc(s("shared_in"), 16)
            sp.dma_start(s3_sb, sw3.rearrange("(c p) n -> p c n", p=P)).then_inc(s("shared_in"), 16)
            sp.dma_start(s2_sb, sw2.rearrange("(c p) n -> p c n", p=P)).then_inc(s("shared_in"), 16)
            for e in range(6):
                load_expert(sp, e, "exp_in")
            sp.wait_ge(s("oT_mm"), GROUPS)
            sp.wait_ge(s("a_rdy"), 4 * GROUPS)
            for e in range(6, 8):
                load_expert(sp, e, "exp67_in")
            sp.wait_ge(s("scat"), 16 * 2 * TILES)
            sp.wait_ge(s("op_mm"), TILES)

            def load(b, a):
                sp.dma_start(xblk[:, a, :], slots_x[bass.ds(b * P, P), :]).then_inc(s(f"x_in{a}"), 16)

            def store(b, a):
                sp.wait_ge(s("by_ev"), b + 1)
                sp.dma_start(slots_y[bass.ds(b * P, P), :], ysb[:, a, :]).then_inc(s(f"y_st{a}"), 16)
            load(0, 0)
            load(1, 1)
            sp.wait_ge(s("bx_tr"), 1)
            load(2, 0)
            with sp.Fori(0, (BLOCKS - 3) // 2) as i:
                for a in (0, 1):
                    sp.wait_ge(s("bx_tr"), 2 * i + a + 2)
                    load(2 * i + a + 3, 1 - a)
                    store(2 * i + a, a)
            for b in range(BLOCKS - 3, BLOCKS):
                store(b, b % 2)
            for T in range(TILES):
                sp.wait_ge(s("comb"), T + 1)
                for w in range(2):
                    sp.dma_start(outv[T, w], hres[64 * w:64 * w + 64, T, :]).then_inc(s("out_s"), 16)
            sp.wait_ge(s("out_s"), 32 * TILES)

        @block.gpsimd
        def _(pool):
            n = [0]

            def step(ins):
                n[0] += 1
                ins.then_inc(s("pool_step"), 1)
                pool.wait_ge(s("pool_step"), n[0])
            nc.gpsimd.memset(xh2[:, :, :], 0.0)
            nc.gpsimd.memset(ident[:, :], 0.0)
            nc.gpsimd.memset(tri[:, :], 1.0)
            nc.gpsimd.memset(ones[:, :], 1.0)
            nc.gpsimd.memset(one[:, :], 1.0)
            nc.gpsimd.memset(eps[:, :], LN_EPS)
            nc.gpsimd.memset(even[:, :], 0.0)
            nc.gpsimd.memset(odd[:, :], HD ** -0.5)
            nc.gpsimd.memset(x1T[:, :, TOK:GPAD], 0.0)
            nc.gpsimd.memset(vaug[:, :, :, HD:HD + 1], 1.0)
            for e in range(E):
                nc.gpsimd.memset(rank[:, :, e:e + 1], float(E - e))
            for t in range(TILES):
                nc.gpsimd.memset(thr[:, :, t:t + 1], float(P * t))
            for b in range(BLOCKS):
                nc.gpsimd.memset(bidx[:, b, :], float(b))
            step(nc.gpsimd.memset(amask[:, :], 1.0))
            step(nc.gpsimd.affine_select(out=ident[:, :], in_=ident[:, :], compare_op=ALU.not_equal, fill=1.0,
                                         base=0, pattern=[[-1, P]], channel_multiplier=1))
            step(nc.gpsimd.affine_select(out=tri[:, :], in_=tri[:, :], compare_op=ALU.is_gt, fill=0.0,
                                         base=0, pattern=[[1, P]], channel_multiplier=-1))
            for r in range(4):
                step(nc.gpsimd.memset(even[32 * r:32 * r + HD, :], HD ** -0.5))
                step(nc.gpsimd.memset(odd[32 * r:32 * r + HD, :], 0.0))
            step(nc.gpsimd.affine_select(out=amask[0:GT, :], in_=amask[0:GT, :], compare_op=ALU.is_ge, fill=0.0,
                                         base=0, pattern=[[1, GT]], channel_multiplier=-1))
            nc.gpsimd.affine_select(out=amask[0:GT, :].rearrange("p (i q) -> p i q", i=GIMG),
                                    in_=amask[0:GT, :].rearrange("p (i q) -> p i q", i=GIMG),
                                    compare_op=ALU.is_ge, fill=0.0, base=0,
                                    pattern=[[-SEQ, GIMG], [0, SEQ]], channel_multiplier=1).then_inc(s("consts"), 1)
            sv = slots_x.rearrange("(n p) d -> p n d", p=P)
            for a in range(0, BLOCKS, TILES):
                k = min(TILES, BLOCKS - a)
                pool.dma_start(sv[:, a:a + k, :], xh2[:, 0:k, :]).then_inc(s("zero_done"), 16)
            for w in range(2):
                for G in range(3):
                    for b in range(2):
                        r0 = PER_SIDE * (3 * b + G) + w
                        pool.dma_start(hres[64 * w + b:64 * w + 64:2, 3 * G:3 * G + 3, :],
                                       pos_emb[r0:r0 + 5:2, :].unsqueeze(0).to_broadcast([32, 3, D])
                                       ).then_inc(s("pos_in"), 16)
            pool.dma_start(bias_b[:, :], b_proj.unsqueeze(0).to_broadcast([P, D])).then_inc(s("bias_in"), 16)

            def stage_group(g, a):
                nc.gpsimd.tensor_copy(xg[:, a], x1T[:, :, bass.ds(g * GT, GT)]).then_inc(s("xg_c"), 1)
            pool.wait_ge(s("x_ev"), TILES)
            stage_group(0, 0)
            stage_group(1, 1)
            with pool.Fori(0, (GROUPS - 3) // 2) as i:
                for a in (0, 1):
                    pool.wait_ge(s("v_mm"), 2 * i + a + 1)
                    stage_group(2 * i + a + 2, a)
            pool.wait_ge(s("v_mm"), GROUPS - 2)
            stage_group(GROUPS - 1, 0)

            pool.wait_ge(s("slot_s"), 1)
            pool.wait_ge(s("zero_done"), 48)
            for T in range(TILES):
                for k in range(2):
                    pool.indirect_dma_start(slots_x, bass.IndirectOffsetOnAxis(slot[:, k, T:T + 1], 0),
                                            xh2[:, T, :], None).then_inc(s("scat"), 16)
            pool.wait_ge(s("y_st0"), 16 * ((BLOCKS + 1) // 2))
            pool.wait_ge(s("y_st1"), 16 * (BLOCKS // 2))
            for T in range(TILES):
                for k in range(2):
                    pool.indirect_dma_start(yg[:, T, k, :], None, slots_y,
                                            bass.IndirectOffsetOnAxis(slot[:, k, T:T + 1], 0)).then_inc(s("gat"), 16)

        @block.scalar
        def _(act):
            act.wait_ge(s("w_tr"), 1)
            for i in range(3):
                nc.scalar.copy(wprojT[:, 2 * i:2 * i + 2, :].rearrange("p c n -> p (c n)"), bank[i][:, :])
            for m in range(4):
                nc.scalar.copy(wT[:, m].rearrange("p c n -> p (c n)"), bank[3 + m][:, :])
            nc.scalar.copy(gateT[:, :, :].rearrange("p c e -> p (c e)"),
                           bank[7][:, 0:DC * E]).then_inc(s("w_ev"), 1)

            def ev_a(T, sl):
                act.wait_ge(s("px_tr"), T + 1)
                nc.scalar.copy(pxT[:, sl, 0:4, :].rearrange("p c q -> p (c q)"), bank[2 * sl][:, :]).then_inc(s("ev_a"), 1)

            def sd(T, sl):
                act.wait_ge(s("ag"), T + 1)
                nc.scalar.activation(std[:, sl:sl + 1], mv[:, sl, 1:2], ACT.Sqrt, bias=eps[:, :]).then_inc(s("sd"), 1)

            def x_ev(T, sl):
                act.wait_ge(s("x_tr"), T + 1)
                dst = x1T[:, :, 0:TOK].rearrange("p c (j t w) -> p c t w j", t=TILES, w=2)
                for c in range(DC):
                    ins = nc.scalar.copy(dst[:, c, bass.ds(T, 1), :, :].rearrange("p t w j -> p (t w) j"),
                                         bank[7][:, c * P:(c + 1) * P].rearrange("p (w j) -> p w j", w=2))
                ins.then_inc(s("x_ev"), 1)
            act.wait_ge(s("consts"), 1)
            with act.Fori(0, 3) as G:
                ev_a(3 * G, 0)
                ev_a(3 * G + 1, 1)
                sd(3 * G, 0)
                ev_a(3 * G + 2, 2)
                sd(3 * G + 1, 1)
                x_ev(3 * G, 0)
                sd(3 * G + 2, 2)
                x_ev(3 * G + 1, 1)
                x_ev(3 * G + 2, 2)

            def qk_ev(g, a):
                act.wait_ge(s("qk_mm"), g + 1)
                b = bank[0][:, 0:4 * GT].rearrange("p (m q) -> p m q", m=4)
                nc.scalar.activation(qk[:, a, 0:2, :], b[:, 0:2, :], ACT.Copy, scale=even[:, :])
                nc.scalar.activation(qk[:, a, 2:4, :], b[:, 0:2, :], ACT.Copy, scale=odd[:, :])
                nc.scalar.copy(qk[:, a, 4:6, :], b[:, 2:4, :]).then_inc(s("qk_ev"), 1)

            def squares(g, a):
                for r in range(4):
                    act.wait_ge(s("s_mm"), 4 * g + r + 1)
                    nc.scalar.activation(probs[0:GT, a, 4 * r:4 * r + 4, :],
                                         bank[2 + r][0:GT, 0:4 * GT].rearrange("p (h q) -> p h q", h=4),
                                         ACT.Square, bias=one[0:GT, :]).then_inc(s("sq"), 1)

            def oT_ev(g, nj):
                act.wait_ge(s("oT_mm"), g + 1)
                for c in range(DC):
                    for w in range(2):
                        src = bank[7][:, c * GT:(c + 1) * GT].rearrange("p (j t w) -> p t w j", t=TILES, w=2)
                        ins = nc.scalar.copy(oT[:, c, :, w, bass.ds(6 * g, nj)], src[:, :, w, 0:nj])
                ins.then_inc(s("oT_ev"), 1)
            with act.Fori(0, GROUPS // 2) as i:
                qk_ev(2 * i, 0)
                squares(2 * i, 0)
                qk_ev(2 * i + 1, 1)
                squares(2 * i + 1, 1)
                oT_ev(2 * i, 6)
                oT_ev(2 * i + 1, 6)
            qk_ev(GROUPS - 1, 0)
            squares(GROUPS - 1, 0)
            oT_ev(GROUPS - 1, 64 - 6 * (GROUPS - 1))

            def sd2(T):
                act.wait_ge(s("ag2"), T + 1)
                nc.scalar.activation(std[:, T:T + 1], mv[:, T, 1:2], ACT.Sqrt, bias=eps[:, :]).then_inc(s("sd2"), 1)

            def x2_ev(T):
                act.wait_ge(s("x2_tr"), T + 1)
                nc.scalar.copy(x2T[:, T, :, :].rearrange("p c q -> p (c q)"),
                               bank[2 + T % 2][:, 0:D]).then_inc(s("x2_ev"), 1)
            for T in range(TILES):
                sd2(T)
                x2_ev(T)
            act.wait_ge(s("rt"), 2)
            nc.scalar.activation(ex, ldiff, ACT.Exp).then_inc(s("ex_s"), 1)

            def g_act(T):
                act.wait_ge(s("g_mm"), T + 1)
                if T:
                    act.wait_ge(s("g_mul"), T)
                nc.scalar.activation(gate[:, 0:SHID], bank[2 * (T % 2)][:, 0:SHID], ACT.Silu).then_inc(s("g_act"), 1)

            def g_ev(T):
                act.wait_ge(s("g_tr"), T + 1)
                nc.scalar.copy(hidT[:, 0:SHC, :].rearrange("p c q -> p (c q)"),
                               bank[6][:, 0:SHID]).then_inc(s("g_ev"), 1)
            g_act(0)
            for T in range(TILES):
                if T + 1 < TILES:
                    g_act(T + 1)
                g_ev(T)

            def bx_ev(b):
                act.wait_ge(s("bx_tr"), b + 1)
                nc.scalar.copy(xT[:, :, :].rearrange("p c q -> p (c q)"), bank[7][:, 0:D]).then_inc(s("bx_ev"), 1)

            def silu(b):
                for i in range(2):
                    act.wait_ge(s(f"bg{i}"), b + 1)
                    nc.scalar.activation(gate[:, i * HALF:(i + 1) * HALF], bank[2 * i][:, 0:HALF],
                                         ACT.Silu).then_inc(s(f"ba{i}"), 1)

            def bh_ea(b):
                act.wait_ge(s("bh_tr"), b + 1)
                nc.scalar.copy(hidT[:, 0:4, :].rearrange("p c q -> p (c q)"), bank[4][:, :]).then_inc(s("bh_ea"), 1)
            bx_ev(0)
            with act.Fori(0, BLOCKS - 1) as b:
                silu(b)
                bx_ev(b + 1)
                bh_ea(b)
            silu(BLOCKS - 1)
            bh_ea(BLOCKS - 1)

        @block.vector
        def _(dve):
            v = nc.vector
            dve.wait_ge(s("pos_in"), 16 * 12)
            dve.wait_ge(s("bias_in"), 16)
            v.tensor_tensor(hres[:, :, :], hres[:, :, :], bias_b[:, :].unsqueeze(1).to_broadcast([P, TILES, D]),
                            ALU.add).then_inc(s("pb_add"), 1)
            dve.wait_ge(s("pb_add"), 1)

            def ev_b(T, sl):
                dve.wait_ge(s("px_tr"), T + 1)
                v.tensor_copy(pxT[:, sl, 4:6, :].rearrange("p c q -> p (c q)"),
                              bank[2 * sl + 1][:, 0:D]).then_inc(s("ev_b"), 1)

            def residual(T, sl):
                dve.wait_ge(s("h_mm"), T + 1)
                h = hres[:, bass.ds(T, 1), :].rearrange("p t d -> p (t d)")
                v.tensor_tensor(h, h, bank[6][:, 0:D], ALU.add).then_inc(s("h_res"), 1)
                dve.wait_ge(s("h_res"), T + 1)
                v.bn_stats(stats[:, sl, :], h).then_inc(s("st"), 1)
                dve.wait_ge(s("st"), T + 1)
                v.bn_aggr(mv[:, sl, :], stats[:, sl, :]).then_inc(s("ag"), 1)

            def norm(T, sl):
                dve.wait_ge(s("sd"), T + 1)
                v.reciprocal(rstd[:, sl:sl + 1], std[:, sl:sl + 1]).then_inc(s("rs"), 1)
                dve.wait_ge(s("rs"), T + 1)
                v.tensor_scalar(xh1[:, sl, :], hres[:, bass.ds(T, 1), :].rearrange("p t d -> p (t d)"),
                                mv[:, sl, 0:1], rstd[:, sl:sl + 1], ALU.subtract, ALU.mult).then_inc(s("xh"), 1)
            for G in range(3):
                ev_b(3 * G, 0)
                ev_b(3 * G + 1, 1)
                residual(3 * G, 0)
                ev_b(3 * G + 2, 2)
                norm(3 * G, 0)
                residual(3 * G + 1, 1)
                norm(3 * G + 1, 1)
                residual(3 * G + 2, 2)
                norm(3 * G + 2, 2)

            def v_ev(g, a):
                dve.wait_ge(s("v_mm"), g + 1)
                v.tensor_copy(vaug[0:GT, a, :, 0:HD],
                              bank[1][0:GT, 0:D].rearrange("p (h d) -> p h d", h=HEADS)).then_inc(s("v_ev"), 1)

            def masked(g, a):
                for r in range(4):
                    dve.wait_ge(s("sq"), 4 * g + r + 1)
                    pr = probs[0:GT, a, 4 * r:4 * r + 4, :]
                    v.scalar_tensor_tensor(pr, pr, 1.0, amask[0:GT, :].unsqueeze(1).to_broadcast([GT, 4, GT]),
                                           ALU.add, ALU.mult).then_inc(s("a_rdy"), 1)

            def o_norm(g, a):
                dve.wait_ge(s("o_mm"), g + 1)
                ov = bank[6][0:GT, 0:HEADS * (HD + 1)].rearrange("p (h d) -> p h d", h=HEADS)
                v.tensor_scalar(zz[0:GT, a, :], ov[:, :, HD], 2 * ATT_EPS, None, ALU.add).then_inc(s("o_z"), 1)
                dve.wait_ge(s("o_z"), g + 1)
                v.reciprocal(rz[0:GT, a, :], zz[0:GT, a, :]).then_inc(s("o_r"), 1)
                dve.wait_ge(s("o_r"), g + 1)
                v.tensor_tensor(onorm[0:GT, a, :].rearrange("p (h d) -> p h d", h=HEADS), ov[:, :, 0:HD],
                                rz[0:GT, a, :].unsqueeze(2).to_broadcast([GT, HEADS, HD]), ALU.mult).then_inc(s("o_n"), 1)
            dve.wait_ge(s("consts"), 1)
            with dve.Fori(0, GROUPS // 2) as i:
                v_ev(2 * i, 0)
                masked(2 * i, 0)
                v_ev(2 * i + 1, 1)
                o_norm(2 * i, 0)
                masked(2 * i + 1, 1)
                o_norm(2 * i + 1, 1)
            v_ev(GROUPS - 1, 0)
            masked(GROUPS - 1, 0)
            o_norm(GROUPS - 1, 0)

            dve.wait_ge(s("zero_done"), 48)
            for T in range(TILES):
                dve.wait_ge(s("op_mm"), T + 1)
                h = hres[:, T, :]
                v.tensor_tensor(h, h, bank[T % 2][:, 0:D], ALU.add).then_inc(s("op_res"), 1)
                dve.wait_ge(s("op_res"), T + 1)
                v.bn_stats(stats[:, T, :], h).then_inc(s("st2"), 1)
                dve.wait_ge(s("st2"), T + 1)
                v.bn_aggr(mv[:, T, :], stats[:, T, :]).then_inc(s("ag2"), 1)
                dve.wait_ge(s("sd2"), T + 1)
                v.reciprocal(rstd[:, T:T + 1], std[:, T:T + 1]).then_inc(s("rs2"), 1)
                dve.wait_ge(s("rs2"), T + 1)
                v.tensor_scalar(xh2[:, T, :], h, mv[:, T, 0:1], rstd[:, T:T + 1],
                                ALU.subtract, ALU.mult).then_inc(s("xh2_s"), 1)

            n = [0]

            def step(ins):
                n[0] += 1
                ins.then_inc(s("rt"), 1)
                dve.wait_ge(s("rt"), n[0])

            def bc(col):
                return col.unsqueeze(2).to_broadcast([P, TILES, E])

            dve.wait_ge(s("lg_mm"), TILES)
            lg = bank[4][:, 0:TILES * E].rearrange("p (t e) -> p t e", e=E)
            step(v.tensor_reduce(lmax, lg, AX.X, ALU.max))
            step(v.tensor_tensor(ldiff, lg, bc(lmax), ALU.subtract))
            dve.wait_ge(s("ex_s"), 1)
            step(v.tensor_reduce(esum, ex, AX.X, ALU.add))
            step(v.reciprocal(rsum, esum))
            step(v.tensor_tensor(score, ex, bc(rsum), ALU.mult))
            step(v.tensor_reduce(w_1, score, AX.X, ALU.max))
            step(v.tensor_tensor(eq1, score, bc(w_1), ALU.is_equal))
            step(v.tensor_tensor(cand1, eq1, rank[:, :, :], ALU.mult))
            step(v.tensor_reduce(best1, cand1, AX.X, ALU.max))
            step(v.tensor_tensor(sel1, cand1, bc(best1), ALU.is_equal))
            step(v.scalar_tensor_tensor(score2, sel1, -2.0, score, ALU.mult, ALU.add))
            step(v.tensor_reduce(w_2, score2, AX.X, ALU.max))
            step(v.tensor_tensor(eq2, score2, bc(w_2), ALU.is_equal))
            step(v.tensor_tensor(cand2, eq2, rank[:, :, :], ALU.mult))
            step(v.tensor_reduce(best2, cand2, AX.X, ALU.max))
            step(v.tensor_tensor(sel2, cand2, bc(best2), ALU.is_equal))
            v.tensor_tensor(sel, sel1, sel2, ALU.add).then_inc(s("sel_s"), 1)
            v.tensor_copy(wts[:, 0, :], w_1)
            v.tensor_copy(wts[:, 1, :], w_2)
            v.memset(tsum[0][:, 0:8, :], 0.0)
            v.memset(tsum[1][:, 0:8, :], 0.0)
            v.memset(csum[0][:, 0:8], 0.0)
            v.memset(csum[1][:, 0:8], 0.0)
            dve.wait_ge(s("pre_mm"), 1)
            step(v.tensor_copy(tsum[0][:, 8:, :], bank[5][:, P:P + TILES * E].rearrange("p (t e) -> p t e", e=E)))
            cur = 0
            for d in (1, 2, 4, 8):
                step(v.tensor_tensor(tsum[1 - cur][:, 8:, :], tsum[cur][:, 8:, :],
                                     tsum[cur][:, 8 - d:8 - d + TILES, :], ALU.add))
                cur = 1 - cur
            incl = tsum[cur]
            step(v.tensor_tensor(cmp_n, incl[:, 7 + TILES, :].unsqueeze(2).to_broadcast([P, E, TILES]),
                                 thr[:, :, :], ALU.is_gt))
            step(v.tensor_reduce(csum[0][:, 8:], cmp_n, AX.X, ALU.add))
            cc = 0
            for d in (1, 2, 4):
                step(v.tensor_tensor(csum[1 - cc][:, 8:], csum[cc][:, 8:], csum[cc][:, 8 - d:8 - d + E], ALU.add))
                cc = 1 - cc
            ends = csum[cc]
            step(v.tensor_tensor(pos, bank[5][:, 0:TILES * E].rearrange("p (t e) -> p t e", e=E),
                                 incl[:, 7:7 + TILES, :], ALU.add))
            step(v.scalar_tensor_tensor(pos, ends[:, 7:7 + E].unsqueeze(1).to_broadcast([P, TILES, E]),
                                        float(P), pos, ALU.mult, ALU.add))
            v.tensor_tensor(ps1, pos, sel1, ALU.mult)
            step(v.tensor_tensor(ps2, pos, sel2, ALU.mult))
            v.tensor_reduce(slot1f, ps1, AX.X, ALU.add)
            step(v.tensor_reduce(slot2f, ps2, AX.X, ALU.add))
            v.tensor_copy(slot[:, 0, :], slot1f)
            v.tensor_copy(slot[:, 1, :], slot2f).then_inc(s("slot_s"), 1)
            step(v.tensor_tensor(cmp_b, ends[:, 8:].unsqueeze(1).to_broadcast([P, BLOCKS, E]),
                                 bidx[:, :, :], ALU.is_le))
            step(v.tensor_reduce(blkf, cmp_b, AX.X, ALU.add))
            v.tensor_scalar(blk[:, :], blkf, float(E - 1), None, ALU.min).then_inc(s("blk_s"), 1)

            def g_mul(T):
                dve.wait_ge(s("g_act"), T + 1)
                if T:
                    dve.wait_ge(s("g_tr"), T)
                v.tensor_tensor(hid[:, 0:SHID], gate[:, 0:SHID], bank[2 * (T % 2) + 1][:, 0:SHID],
                                ALU.mult).then_inc(s("g_mul"), 1)

            def y_add(T):
                dve.wait_ge(s("y_mm"), T + 1)
                v.tensor_tensor(hres[:, T, :], hres[:, T, :], bank[7][:, 0:D], ALU.add).then_inc(s("y_add"), 1)
            g_mul(0)
            for T in range(TILES):
                if T + 1 < TILES:
                    g_mul(T + 1)
                y_add(T)

            def mul(b):
                for i in range(2):
                    dve.wait_ge(s(f"ba{i}"), b + 1)
                    ins = v.tensor_tensor(hid[:, i * HALF:(i + 1) * HALF], gate[:, i * HALF:(i + 1) * HALF],
                                          bank[2 * i + 1][:, 0:HALF], ALU.mult)
                ins.then_inc(s("bm"), 1)

            def y_ev(b, a, stored):
                if stored is not None:
                    dve.wait_ge(s(f"y_st{a}"), stored)
                dve.wait_ge(s("by_mm"), b + 1)
                v.tensor_copy(ysb[:, a, :], bank[6][:, 0:D]).then_inc(s("by_ev"), 1)

            def bh_eb(b):
                dve.wait_ge(s("bh_tr"), b + 1)
                v.tensor_copy(hidT[:, 4, :], bank[5][:, 0:P])
                v.tensor_copy(hidT[0:HLAST, 5, :], bank[5][0:HLAST, P:2 * P]).then_inc(s("bh_eb"), 1)
            for b in range(3):
                mul(b)
                if b:
                    y_ev(b - 1, (b - 1) % 2, None)
                bh_eb(b)
            with dve.Fori(0, (BLOCKS - 3) // 2) as i:
                for a in (0, 1):
                    mul(2 * i + a + 3)
                    y_ev(2 * i + a + 2, a, 16 * i + 16)
                    bh_eb(2 * i + a + 3)
            y_ev(BLOCKS - 1, 0, 16 * ((BLOCKS - 1) // 2))

            for T in range(TILES):
                dve.wait_ge(s("gat"), 32 * TILES if T == 0 else 32 * TILES)
                for k in range(2):
                    if k:
                        dve.wait_ge(s("rt"), n[0])
                    ins = v.scalar_tensor_tensor(hres[:, T, :], yg[:, T, k, :], wts[:, k, T:T + 1], hres[:, T, :],
                                                 ALU.mult, ALU.add)
                    if k == 0:
                        n[0] += 1
                        ins.then_inc(s("rt"), 1)
                ins.then_inc(s("comb"), 1)

        @block.tensor
        def _(pe):
            t = nc.tensor
            pe.wait_ge(s("consts"), 1)
            pe.wait_ge(s("wproj_in"), 16)
            for c in range(DC):
                for k in range(PDC):
                    t.transpose(bank[k // 2][:, (k % 2) * D + c * P:(k % 2) * D + (c + 1) * P],
                                wproj_nat[:, c, k * P:(k + 1) * P], ident[:, :])
            pe.wait_ge(s("w_in"), 64)
            for m in range(4):
                for c in range(DC):
                    for k in range(DC):
                        t.transpose(bank[3 + m][:, k * D + c * P:k * D + (c + 1) * P],
                                    w_nat[:, m, c, k * P:(k + 1) * P], ident[:, :])
            pe.wait_ge(s("gate_in"), 16)
            for k in range(DC):
                ins = t.transpose(bank[7][:, k * E:(k + 1) * E], gnat[:, k * P:(k + 1) * P], ident[0:E, 0:E])
            ins.then_inc(s("w_tr"), 1)
            pe.wait_ge(s("w_ev"), 1)

            def tr(G, sl):
                pe.wait_ge(s(f"px_in{sl}"), 32 * G + 32)
                for k in range(PDC):
                    ins = t.transpose(bank[2 * sl + k // 4][:, (k % 4) * P:(k % 4 + 1) * P],
                                      px[:, sl, k * P:(k + 1) * P], ident[:, :])
                ins.then_inc(s("px_tr"), 1)

            def mm(T, sl):
                pe.wait_ge(s("ev_a"), T + 1)
                pe.wait_ge(s("ev_b"), T + 1)
                if sl:
                    pe.wait_ge(s("h_res"), T)
                for k in range(PDC):
                    ins = t.matmul(bank[6][:, 0:D], pxT[:, sl, k, :], wprojT[:, k, :], start=(k == 0), stop=(k == PDC - 1))
                ins.then_inc(s("h_mm"), 1)

            def xt(T, sl):
                pe.wait_ge(s("xh"), T + 1)
                if sl:
                    pe.wait_ge(s("x_ev"), T)
                for k in range(DC):
                    ins = t.transpose(bank[7][:, k * P:(k + 1) * P], xh1[:, sl, k * P:(k + 1) * P], ident[:, :])
                ins.then_inc(s("x_tr"), 1)
            with pe.Fori(0, 3) as G:
                tr(G, 0)
                tr(G, 1)
                mm(3 * G, 0)
                tr(G, 2)
                mm(3 * G + 1, 1)
                xt(3 * G, 0)
                mm(3 * G + 2, 2)
                xt(3 * G + 1, 1)
                xt(3 * G + 2, 2)

            def project(g, a):
                pe.wait_ge(s("xg_c"), g + 1)
                for m in range(2):
                    for c in range(DC):
                        for k in range(DC):
                            ins = t.matmul(bank[0][:, (2 * m + c) * GT:(2 * m + c + 1) * GT],
                                           wT[:, m, k, c * P:(c + 1) * P], xg[:, a, k, :],
                                           start=(k == 0), stop=(k == DC - 1))
                ins.then_inc(s("qk_mm"), 1)
                if a:
                    pe.wait_ge(s("v_ev"), g)
                for k in range(DC):
                    ins = t.matmul(bank[1][0:GT, 0:D], xg[:, a, k, :], wT[:, 2, k, :], start=(k == 0), stop=(k == DC - 1))
                ins.then_inc(s("v_mm"), 1)

            def scores(g, a):
                pe.wait_ge(s("qk_ev"), g + 1)
                for r in range(4):
                    for c in range(DC):
                        for par in range(2):
                            h = 2 * c + par
                            ins = t.matmul(bank[2 + r][0:GT, h * GT:(h + 1) * GT],
                                           qk[32 * r:32 * r + 32, a, 4 + c, :],
                                           qk[32 * r:32 * r + 32, a, 2 * par + c, :], start=True, stop=True)
                    ins.then_inc(s("s_mm"), 1)

            def values(g, a):
                pe.wait_ge(s("v_ev"), g + 1)
                for r in range(4):
                    pe.wait_ge(s("a_rdy"), 4 * g + r + 1)
                    for i in range(4):
                        h = 8 * (i // 2) + 2 * r + i % 2
                        ins = t.matmul(bank[6][0:GT, h * (HD + 1):(h + 1) * (HD + 1)], probs[0:GT, a, 4 * r + i, :],
                                       vaug[0:GT, a, h, :], start=True, stop=True)
                ins.then_inc(s("o_mm"), 1)

            def turn_o(g, a):
                pe.wait_ge(s("o_n"), g + 1)
                if a:
                    pe.wait_ge(s("oT_ev"), g)
                for k in range(DC):
                    ins = t.transpose(bank[7][:, k * GT:(k + 1) * GT], onorm[0:GT, a, k * P:(k + 1) * P],
                                      ident[0:GT, 0:GT])
                ins.then_inc(s("oT_mm"), 1)
            with pe.Fori(0, GROUPS // 2) as i:
                project(2 * i, 0)
                scores(2 * i, 0)
                project(2 * i + 1, 1)
                values(2 * i, 0)
                scores(2 * i + 1, 1)
                turn_o(2 * i, 0)
                values(2 * i + 1, 1)
                turn_o(2 * i + 1, 1)
            g = GROUPS - 1
            project(g, 0)
            scores(g, 0)
            values(g, 0)
            turn_o(g, 0)

            pe.wait_ge(s("oT_ev"), GROUPS)

            def oproj(T):
                if T >= 2:
                    pe.wait_ge(s("op_res"), T - 1)
                for k in range(DC):
                    ins = t.matmul(bank[T % 2][:, 0:D], oT[:, k, T, :, :].rearrange("p w j -> p (w j)"), wT[:, 3, k, :],
                                   start=(k == 0), stop=(k == DC - 1))
                ins.then_inc(s("op_mm"), 1)

            def x2t(T):
                pe.wait_ge(s("xh2_s"), T + 1)
                for k in range(DC):
                    ins = t.transpose(bank[2 + T % 2][:, k * P:(k + 1) * P], xh2[:, T, k * P:(k + 1) * P], ident[:, :])
                ins.then_inc(s("x2_tr"), 1)

            def logits(T):
                pe.wait_ge(s("x2_ev"), T + 1)
                for k in range(DC):
                    ins = t.matmul(bank[4][:, T * E:(T + 1) * E], x2T[:, T, k, :], gateT[:, k, :],
                                   start=(k == 0), stop=(k == DC - 1))
                ins.then_inc(s("lg_mm"), 1)
            oproj(0)
            for T in range(TILES):
                if T + 1 < TILES:
                    oproj(T + 1)
                x2t(T)
                if T:
                    logits(T - 1)
            logits(TILES - 1)
            pe.wait_ge(s("sel_s"), 1)
            selr = sel.rearrange("p t e -> p (t e)")
            t.matmul(bank[5][:, 0:TILES * E], tri[:, :], selr, start=True, stop=True)
            t.matmul(bank[5][:, P:P + TILES * E], ones[:, :], selr, start=True, stop=True).then_inc(s("pre_mm"), 1)

            pe.wait_ge(s("shared_in"), 48)

            def s_up(T):
                if T >= 2:
                    pe.wait_ge(s("g_mul"), T - 1)
                for i, w in enumerate((s1_sb, s3_sb)):
                    for k in range(DC):
                        ins = t.matmul(bank[2 * (T % 2) + i][:, 0:SHID], x2T[:, T, k, :], w[:, k, :],
                                       start=(k == 0), stop=(k == DC - 1))
                ins.then_inc(s("g_mm"), 1)

            def s_turn(T):
                pe.wait_ge(s("g_mul"), T + 1)
                if T:
                    pe.wait_ge(s("g_ev"), T)
                for k in range(SHC):
                    ins = t.transpose(bank[6][:, k * P:(k + 1) * P], hid[:, k * P:(k + 1) * P], ident[:, :])
                ins.then_inc(s("g_tr"), 1)

            def s_down(T):
                pe.wait_ge(s("g_ev"), T + 1)
                if T:
                    pe.wait_ge(s("y_add"), T)
                for k in range(SHC):
                    ins = t.matmul(bank[7][:, 0:D], hidT[:, k, :], s2_sb[:, k, :], start=(k == 0), stop=(k == SHC - 1))
                ins.then_inc(s("y_mm"), 1)
            s_up(0)
            for T in range(TILES):
                if T + 1 < TILES:
                    s_up(T + 1)
                s_turn(T)
                s_down(T)

            pe.wait_ge(s("y_add"), TILES)
            pe.wait_ge(s("blk_s"), 1)
            pe.wait_ge(s("exp_in"), 16 * 4 * 6)
            pe.wait_ge(s("exp67_in"), 16 * 4 * 2)

            def bx(b, a, count):
                pe.wait_ge(s(f"x_in{a}"), count)
                for k in range(DC):
                    ins = t.transpose(bank[7][:, k * P:(k + 1) * P], xblk[:, a, k * P:(k + 1) * P], ident[:, :])
                ins.then_inc(s("bx_tr"), 1)

            def expert_of(b):
                return pe.value_load(blk[0:1, bass.ds(b, 1)], min_val=0, max_val=E - 1)

            def up(b):
                e = expert_of(b)
                pe.wait_ge(s("bx_ev"), b + 1)
                for i in range(2):
                    for j, base in enumerate((W1, W3)):
                        for k in range(DC):
                            ins = t.matmul(bank[2 * i + j][:, 0:HALF], xT[:, k, :],
                                           experts[:, bass.ds(e * WEXP + (base + k * HID + i * HALF), HALF)],
                                           start=(k == 0), stop=(k == DC - 1))
                    ins.then_inc(s(f"bg{i}"), 1)

            def bturn(b):
                pe.wait_ge(s("bm"), b + 1)
                for k in range(HC):
                    m = P if k < HC - 1 else HLAST
                    ins = t.transpose(bank[4 + k // 4][0:m, (k % 4) * P:(k % 4 + 1) * P], hid[:, k * P:k * P + m],
                                      ident[:, :])
                ins.then_inc(s("bh_tr"), 1)

            def down(b):
                e = expert_of(b)
                pe.wait_ge(s("bh_ea"), b + 1)
                pe.wait_ge(s("bh_eb"), b + 1)
                for k in range(HC):
                    m = P if k < HC - 1 else HLAST
                    ins = t.matmul(bank[6][:, 0:D], hidT[0:m, k, :],
                                   experts[0:m, bass.ds(e * WEXP + (W2 + k * D), D)],
                                   start=(k == 0), stop=(k == HC - 1))
                ins.then_inc(s("by_mm"), 1)
            bx(0, 0, 16)
            up(0)
            bx(1, 1, 16)
            bturn(0)
            with pe.Fori(0, (BLOCKS - 3) // 2) as i:
                for a in (0, 1):
                    b = 2 * i + a + 1
                    up(b)
                    down(b - 1)
                    bx(b + 1, a, 16 * i + (32 if a == 0 else 32))
                    bturn(b)
            up(BLOCKS - 2)
            down(BLOCKS - 3)
            bx(BLOCKS - 1, 0, 16 * ((BLOCKS + 1) // 2))
            bturn(BLOCKS - 2)
            up(BLOCKS - 1)
            down(BLOCKS - 2)
            bturn(BLOCKS - 1)
            down(BLOCKS - 1)


_INS = ["x", "L0_tok_W_proj", "L0_tok_b_proj", "L0_tok_pos_emb", "L0_attn_Wq", "L0_attn_Wk", "L0_attn_Wv", "L0_attn_Wo",
        "L0_ffn_gate_w", "L0_ffn_w1", "L0_ffn_w2", "L0_ffn_w3", "L0_ffn_sw1", "L0_ffn_sw2", "L0_ffn_sw3"]


def kernel(**inputs):
    import numpy as np
    import concourse.bacc as bacc
    from concourse.bass_utils import run_bass_kernel_spmd

    nc = bacc.Bacc("TRN2", target_bir_lowering=False, num_devices=1)
    arrays, args = {}, []
    for name in _INS:
        a = np.ascontiguousarray(inputs[name])
        arrays[f"in_{name}"] = a
        args.append(nc.dram_tensor(f"in_{name}", a.shape, mybir.dt.from_np(a.dtype), kind="ExternalInput").ap())
    args.append(nc.dram_tensor("out_0", (IMAGES, SEQ, D), F32, kind="ExternalOutput").ap())
    vit_moe(nc, *args)
    r = run_bass_kernel_spmd(nc, [arrays], core_ids=[0])
    return r.results[0]["out_0"]
```

```python
from contextlib import ExitStack

import concourse.bass as bass
from concourse import mybir

F32 = mybir.dt.float32
F16 = mybir.dt.float16
I32 = mybir.dt.int32
U32 = mybir.dt.uint32
ALU = mybir.AluOpType
ACT = mybir.ActivationFunctionType
AX = mybir.AxisListType

P = 128
IMAGES, SIDE, CH, PATCH = 32, 96, 3, 16
PER_SIDE = SIDE // PATCH
SEQ = PER_SIDE * PER_SIDE
TOK = IMAGES * SEQ
D = 256
DC = D // P
PD = PATCH * PATCH * CH
PDC = PD // P
RUN = PATCH * CH
TILES = TOK // P
HEADS, HD = 16, 16
VW = 32
GIMG = 3
GT = GIMG * SEQ
GROUPS = -(-IMAGES // GIMG)
GPAD = GROUPS * GT
E, HID, SHID = 8, 704, 384
HALF = HID // 2
HC = -(-HID // P)
HLAST = HID - (HC - 1) * P
SHC = SHID // P
BLOCKS = (2 * TOK + E * (P - 1)) // P
SLOTS = BLOCKS * P
W1, W3, W2, WEXP = 0, DC * HID, 2 * DC * HID, 2 * DC * HID + HC * D
ROW = D + E + 1
SW = 2 * DC * SHID + SHC * D
STAGE = 3 * D
LAST_CHUNKS = 6
WS, XS, HS = 256.0, 256.0, 16.0
PS, AS = 64.0, 64.0
QSCALE = HD ** -0.5 * AS / (XS * WS)
LN_EPS = 1e-5
ATT_EPS = 1e-6


def vit_moe(nc, x, w_proj, b_proj, pos_emb, wq, wk, wv, wo, gate_w, w1, w2, w3, sw1, sw2, sw3, out):
    ctx = ExitStack()
    with ctx:
        def sb(name, shape, dt=F32):
            return ctx.enter_context(nc.sbuf_tensor(name, shape, dt))

        def sem(name):
            return ctx.enter_context(nc.semaphore(name))

        slots_x = nc.dram_tensor("slots_x", [SLOTS, ROW], F32, kind="Internal").ap()
        acc = nc.dram_tensor("acc", [TOK + P, D], F32, kind="Internal").ap()

        experts = sb("experts", [P, E * 2 * WEXP], F16)
        early = experts[:, 6 * 2 * WEXP:].bitcast(F32)
        stage = sb("stage", [P, 2, STAGE])
        px = early[:, 0:3 * PD].rearrange("p (s d) -> p s d", s=3)
        probs = early[:, 0:2 * HEADS * GT].rearrange("p (a h q) -> p a h q", a=2, h=HEADS)
        o = 2 * HEADS * GT
        wproj_nat = early[:, o:o + DC * PD].rearrange("p (c d) -> p c d", c=DC)
        qk = early[:, o:o + 2 * 6 * GT].bitcast(F16).rearrange("p (a h m q) -> p a h m q", a=2, h=2, m=6)
        o += DC * PD
        w_nat = early[:, o:o + 4 * DC * D].rearrange("p (m c d) -> p m c d", m=4, c=DC)
        oraw = early[:, o:o + 4 * GT].rearrange("p (i q) -> p i q", i=4)
        o += 4 * DC * D
        vaug = early[:, o:o + 2 * HEADS * VW].rearrange("p (a h d) -> p a h d", a=2, h=HEADS)
        o += 2 * HEADS * VW
        onorm = early[:, o:o + 2 * D].rearrange("p (a d) -> p a d", a=2)
        o += 2 * D
        shared_w = sb("shared_w", [P, 2, SW], F16)
        xa = sb("xa", [P, DC * GPAD])
        x1T = xa[:, :].bitcast(F16).rearrange("p (h c t) -> p h c t", h=2, c=DC)
        x2T = xa[:, 0:TILES * D].bitcast(F16).rearrange("p (t h c q) -> p t h c q", t=TILES, h=2, c=DC)
        hres = sb("hres", [P, TILES, D])
        xh2 = sb("xh2", [P, TILES, ROW])
        ob = sb("ob", [P, 3 * PD])
        pxT = ob[:, 0:2 * PD].bitcast(F16).rearrange("p (s h q) -> p s h q", s=2, h=2)
        oT = ob[:, :].bitcast(F16).rearrange("p (h c t j) -> p h c t j", h=2, c=DC, t=2 * TILES)
        fw = sb("fw", [P, PDC * D + 4 * DC * D])
        wprojT = fw[:, 0:PDC * D].bitcast(F16).rearrange("p (h q) -> p h q", h=2)
        wT = fw[:, PDC * D:].bitcast(F16).rearrange("p (h m q) -> p h m q", h=2, m=4)
        o = 0
        x2f = fw[:, o:o + 2 * D].rearrange("p (a c q) -> p a c q", a=2, c=DC)
        xblk = fw[:, o:o + 2 * D].rearrange("p (a d) -> p a d", a=2); o += 2 * D
        xT = fw[:, o:o + D].bitcast(F16).rearrange("p (h c q) -> p h c q", h=2, c=DC); o += D
        gate = fw[:, o:o + HID]; o += HID
        hid = fw[:, o:o + HID]; o += HID
        hidT = fw[:, o:o + HC * P].bitcast(F16).rearrange("p (h c q) -> p h c q", h=2, c=HC); o += HC * P
        ysb = fw[:, o:o + 2 * D].rearrange("p (a d) -> p a d", a=2); o += 2 * D
        assert o <= PDC * D + 4 * DC * D
        free = 3 * PD
        xh1 = early[:, free:free + 3 * D].rearrange("p (s d) -> p s d", s=3)
        bias_b = early[:, free + 3 * D:free + 4 * D]
        ident = sb("ident", [P, P])
        tri = sb("tri", [P, P])
        ones = sb("ones", [P, P])
        amask = sb("amask", [P, GT])
        gnat = xh2[0:E, 0, 0:D]
        gateT = sb("gateT", [P, DC, E])
        even = sb("even", [P, 1])
        odd = sb("odd", [P, 1])
        one = sb("one", [P, 1])
        eps = sb("eps", [P, 1])
        stats = sb("stats", [P, TILES, 6])
        mv = sb("mv", [P, TILES, 2])
        std = sb("std", [P, TILES])
        rstd = sb("rstd", [P, TILES])
        rz = sb("rz", [P, 2, HEADS])
        zz = sb("zz", [P, 2, HEADS])
        small = [0]

        def over(n):
            v = ob[:, small[0]:small[0] + n]
            small[0] += n
            assert small[0] <= 3 * PD
            return v

        def te(n=TILES):
            return over(n * E).rearrange("p (t e) -> p t e", e=E)
        rank = sb("rank", [P, E])
        thr = sb("thr", [P, TILES])
        bidx = sb("bidx", [P, BLOCKS])
        tokid = sb("tokid", [P, TILES], I32)
        ldiff, ex, score, eq1, cand1, sel1, score2, eq2, cand2, sel2, sel = [te() for _ in range(11)]
        pos, ps1, ps2 = te(), te(), te()
        tsum = [te(8 + TILES), te(8 + TILES)]
        cmp_n = over(E * TILES).rearrange("p (e t) -> p e t", e=E)
        cmp_b = over(BLOCKS * E).rearrange("p (b e) -> p b e", e=E)
        csum = [over(8 + E), over(8 + E)]
        lmax, esum, rsum, best1, best2, w_1, w_2, slot1f, slot2f = [over(TILES) for _ in range(9)]
        blkf = over(BLOCKS)
        erow = over(BLOCKS * E).rearrange("p (b e) -> p b e", e=E)
        rblk = over(BLOCKS)
        onehot = over(BLOCKS * E).rearrange("p (b e) -> p b e", e=E)
        meta = sb("meta", [P, BLOCKS, E + 1])
        wts = sb("wts", [P, BLOCKS])
        slot = sb("slot", [P, 2, TILES], I32)
        blk = sb("blk", [P, BLOCKS], I32)

        bank = [ctx.enter_context(nc.psum_tensor(f"bank{i}", [P, 512], F32)) for i in range(8)]

        OP = (0, 1, 5, 6)

        S = {}

        def s(name):
            if name not in S:
                S[name] = sem(name)
            return S[name]

        for n in ("wproj_in w_in gate_in bias_in pos_in px_in0 px_in1 px_in2 stage_in0 stage_in1 w_hi w_lo zero_done "
                  "pool_step consts w_tr fw_hi fw_lo gateT_s px_tr px_hi px_lo h_mm h_res st ag sd rs xh x_tr x_hi x_lo "
                  "qk_mm qk_hi qk_lo v_mm v_ev s_mm sq a_rdy o_mm o_raw o_turn o_z o_r o_n oT_mm oT_hi oT_lo pad_z "
                  "op_mm op_res st2 ag2 sd2 rs2 xh2_s x2_tr x2_f x2_hi x2_lo lg_mm rt ex_s pre_mm sel_s slot_s blk_s "
                  "g_mm g_act g_mul g_tr g_hi g_lo y_mm y_add scat x_in0 x_in1 bx_tr bx_hi bx_lo bg0 bg1 ba0 ba1 bm meta_in "
                  "stage_z tok_i bh_tr bh_hi bh_lo by_mm by_ev acc_init acc_add out_s pb_add").split():
            s(n)

        xv = x.rearrange("b (hp ph) w c -> (b hp) ph (w c)", ph=PATCH).rearrange("(j g) ph q -> g j ph q", g=3)
        outv = out.rearrange("b s d -> (b s) d")
        accv = acc[0:TOK, :].rearrange("(j t w) d -> t w j d", t=TILES, w=2)

        block = ctx.enter_context(nc.Block())

        def load_patches(eng, G, W):
            for w in range(2):
                c = (2 * W + w) * RUN
                eng.dma_start(px[64 * w:64 * w + 64, W, :].rearrange("p (a r) -> p a r", a=PATCH),
                              xv[G, :, :, c:c + RUN]).then_inc(s(f"px_in{W}"), 16)

        def expert_chunk(e, c):
            if c < 4:
                w, k = (w1, w3)[c // 2], c % 2
                return c * HID, HID, [(P, 1, 0, HID, w[bass.ds(e, 1), k * P:(k + 1) * P, :].rearrange("e p n -> p e n"))]
            rows = w2[bass.ds(e, 1)]
            if c == 4:
                return W2, 3 * D, [(P, 3, 0, 3 * D, rows[:, 0:3 * P, :].rearrange("e (k p) n -> p (e k) n", p=P))]
            return W2 + 3 * D, 3 * D, [
                (P, 2, 0, 2 * D, rows[:, 3 * P:5 * P, :].rearrange("e (k p) n -> p (e k) n", p=P)),
                (HLAST, 1, 2 * D, 3 * D, rows[:, 5 * P:HID, :].rearrange("e p n -> p e n"))]

        def shared_chunk(c):
            if c < 2:
                return c * DC * SHID, DC * SHID, [(P, DC, 0, DC * SHID, (sw1, sw3)[c].rearrange("(k p) n -> p k n", p=P))]
            k0, k1 = ((0, 2), (2, 3))[c - 2]
            return (2 * DC * SHID + k0 * D, (k1 - k0) * D,
                    [(P, k1 - k0, 0, (k1 - k0) * D, sw2[k0 * P:k1 * P, :].rearrange("(k p) n -> p k n", p=P))])

        def arrived(e, c):
            late = 32 if isinstance(e, int) and e >= 6 else 0
            return e * 48 + 8 * c + 16 + late if c % 2 == 0 else e * 64 + (8 * c + 8 if c < 5 else 64) + late

        def load_chunk(eng, e, c, n, pieces):
            if not isinstance(n, int) or n >= 2:
                eng.wait_ge(s("w_lo"), n - 1)
            for parts, k, lo, hi, src in pieces:
                eng.dma_start(stage[0:parts, c % 2, lo:hi].rearrange("p (k n) -> p k n", k=k),
                              src).then_inc(s(f"stage_in{c % 2}"), 16)

        def load_expert_chunk(eng, e, c):
            n = e * 6 + c + (4 if isinstance(e, int) and e >= 6 else 0)
            load_chunk(eng, e, c, n, expert_chunk(e, c)[2])

        def split_hi(act, dst, size, c, count):
            act.wait_ge(s(f"stage_in{c % 2}"), count)
            nc.scalar.activation(dst, stage[:, c % 2, 0:size], ACT.Copy, scale=WS).then_inc(s("w_hi"), 1)

        def split_lo(dve, dst, hi, size, c, n):
            dve.wait_ge(s("w_hi"), n + 1)
            nc.vector.scalar_tensor_tensor(dst, stage[:, c % 2, 0:size], WS, hi, ALU.mult, ALU.subtract).then_inc(s("w_lo"), 1)

        def expert_at(e, half, off, size):
            return experts[:, bass.ds(e * (2 * WEXP) + (half * WEXP + off), size)]

        def expert_hi(act, e, c):
            off, size, _ = expert_chunk(e, c)
            split_hi(act, expert_at(e, 0, off, size), size, c, arrived(e, c))

        def expert_lo(dve, e, c):
            off, size, _ = expert_chunk(e, c)
            n = e * 6 + c + (4 if isinstance(e, int) and e >= 6 else 0)
            split_lo(dve, expert_at(e, 1, off, size), expert_at(e, 0, off, size), size, c, n)

        def shared_hi(act, c):
            off, size, _ = shared_chunk(c)
            split_hi(act, shared_w[:, 0, off:off + size], size, c,
                     (6 * 48 if c % 2 == 0 else 6 * 64) + 16 * (c // 2) + 16)

        def shared_lo(dve, c):
            off, size, _ = shared_chunk(c)
            split_lo(dve, shared_w[:, 1, off:off + size], shared_w[:, 0, off:off + size], size, c, 36 + c)

        def x1_at(half, c, T):
            return x1T[:, half, c, 0:TOK].rearrange("p (j t w) -> p t w j", t=TILES, w=2)[:, T]

        def turned_o(c, nj):
            return bank[7][:, c * GT:(c + 1) * GT].rearrange("p (j q) -> p q j", j=6)[:, :, 0:nj]

        @block.sync
        def _(sp):
            load_patches(sp, 0, 0)
            sp.dma_start(wproj_nat, w_proj.rearrange("(c p) d -> p c d", p=P)).then_inc(s("wproj_in"), 16)
            for W in range(1, 3):
                load_patches(sp, 0, W)
            sp.wait_ge(s("stage_z"), 1)
            for G in range(1, 3):
                for W in range(3):
                    sp.wait_ge(s("px_tr"), 3 * (G - 1) + W + 1)
                    load_patches(sp, G, W)
                for c in range(2):
                    load_expert_chunk(sp, 0, 2 * (G - 1) + c)
            for c in range(4, 6):
                load_expert_chunk(sp, 0, c)
            with sp.Fori(1, 5) as e:
                for c in range(6):
                    load_expert_chunk(sp, e, c)
            for c in range(6):
                load_expert_chunk(sp, 5, c)
            for c in range(4):
                load_chunk(sp, 6, c, 36 + c, shared_chunk(c)[2])
            for e in range(6, 8):
                for c in range(6):
                    load_expert_chunk(sp, e, c)
            sp.wait_ge(s("scat"), 16 * 2 * TILES)
            sp.dma_start(meta[:, :, :], slots_x.rearrange("(b p) d -> p b d", p=P)[:, :, D:ROW]).then_inc(s("meta_in"), 16)

            def load(b, a):
                sp.dma_start(xblk[:, a, :], slots_x[bass.ds(b * P, P), 0:D]).then_inc(s(f"x_in{a}"), 16)
            load(0, 0)
            load(1, 1)
            with sp.Fori(0, (BLOCKS - 3) // 2) as i:
                for a in (0, 1):
                    sp.wait_ge(s("bx_tr"), 2 * i + a + 1)
                    load(2 * i + a + 2, a)
            sp.wait_ge(s("bx_tr"), BLOCKS - 2)
            load(BLOCKS - 1, 0)
            sp.wait_ge(s("acc_add"), 16 * BLOCKS)
            sp.dma_start(outv, acc[0:TOK, :]).then_inc(s("out_s"), 16)
            sp.wait_ge(s("out_s"), 16)

        @block.gpsimd
        def _(pool):
            n = [0]

            def step(ins):
                n[0] += 1
                ins.then_inc(s("pool_step"), 1)
                pool.wait_ge(s("pool_step"), n[0])
            nc.gpsimd.memset(ident[:, :], 0.0)
            nc.gpsimd.memset(tri[:, :], 1.0)
            nc.gpsimd.memset(ones[:, :], 1.0)
            nc.gpsimd.memset(one[:, :], 1.0)
            nc.gpsimd.memset(eps[:, :], LN_EPS)
            nc.gpsimd.memset(even[:, :], 0.0)
            nc.gpsimd.memset(odd[:, :], QSCALE)
            step(nc.gpsimd.memset(amask[:, :], 1.0))
            step(nc.gpsimd.affine_select(out=ident[:, :], in_=ident[:, :], compare_op=ALU.not_equal, fill=1.0,
                                         base=0, pattern=[[-1, P]], channel_multiplier=1))
            step(nc.gpsimd.affine_select(out=tri[:, :], in_=tri[:, :], compare_op=ALU.is_gt, fill=0.0,
                                         base=0, pattern=[[1, P]], channel_multiplier=-1))
            for r in range(4):
                step(nc.gpsimd.memset(even[32 * r:32 * r + HD, :], QSCALE))
                step(nc.gpsimd.memset(odd[32 * r:32 * r + HD, :], 0.0))
            step(nc.gpsimd.affine_select(out=amask[0:GT, :], in_=amask[0:GT, :], compare_op=ALU.is_ge, fill=0.0,
                                         base=0, pattern=[[1, GT]], channel_multiplier=-1))
            nc.gpsimd.affine_select(out=amask[0:GT, :].rearrange("p (i q) -> p i q", i=GIMG),
                                    in_=amask[0:GT, :].rearrange("p (i q) -> p i q", i=GIMG),
                                    compare_op=ALU.is_ge, fill=0.0, base=0,
                                    pattern=[[-SEQ, GIMG], [0, SEQ]], channel_multiplier=1).then_inc(s("consts"), 1)
            nc.gpsimd.memset(stage[:, :, :], 0.0).then_inc(s("stage_z"), 1)
            for w in range(2):
                for b in range(2):
                    pool.dma_start(hres[64 * w + b:64 * w + 64:2, :, :],
                                   pos_emb[18 * b + w:18 * b + 18:2, :].unsqueeze(0).to_broadcast([32, TILES, D])
                                   ).then_inc(s("pos_in"), 16)
            nc.gpsimd.memset(x1T[:, :, :, TOK:GPAD], 0.0).then_inc(s("pad_z"), 1)
            step(nc.gpsimd.memset(vaug[:, :, :, HD:VW], 0.0))
            nc.gpsimd.memset(vaug[:, :, :, HD:HD + 1], 1.0).then_inc(s("pad_z"), 1)
            for e in range(E):
                nc.gpsimd.memset(rank[:, e:e + 1], float(E - e))
            for t in range(TILES):
                nc.gpsimd.memset(thr[:, t:t + 1], float(P * t))
            for b in range(BLOCKS):
                nc.gpsimd.memset(bidx[:, b:b + 1], float(b))
            nc.gpsimd.iota(tokid[:, :], pattern=[[2, TILES]], base=0, channel_multiplier=18).then_inc(s("tok_i"), 1)
            pool.wait_ge(s("w_tr"), 4)
            step(nc.gpsimd.memset(xh2[:, :, :], 0.0))
            step(nc.gpsimd.iota(xh2[:, :, ROW - 1:ROW].bitcast(I32), pattern=[[0, TILES], [0, 1]], base=TOK,
                                channel_multiplier=1))
            pool.wait_ge(s("px_tr"), TILES)
            sv = slots_x.rearrange("(n p) d -> p n d", p=P)
            for a in range(0, BLOCKS, TILES):
                k = min(TILES, BLOCKS - a)
                pool.dma_start(sv[:, a:a + k, :], xh2[:, 0:k, :]).then_inc(s("zero_done"), 16)
            pool.dma_start(acc[TOK:TOK + P, :], xh2[:, 0, 0:D]).then_inc(s("zero_done"), 16)

            pool.wait_ge(s("slot_s"), 1)
            pool.wait_ge(s("zero_done"), 64)
            for T in range(TILES):
                for k in range(2):
                    pool.indirect_dma_start(slots_x, bass.IndirectOffsetOnAxis(slot[:, k, T:T + 1], 0),
                                            xh2[:, T, :], None).then_inc(s("scat"), 16)
            pool.wait_ge(s("acc_init"), 32 * TILES)
            pool.wait_ge(s("meta_in"), 16)
            for b in range(BLOCKS):
                if b:
                    pool.wait_ge(s("acc_add"), 16 * b)
                pool.wait_ge(s("by_ev"), b + 1)
                pool.indirect_dma_start(acc, bass.IndirectOffsetOnAxis(meta[:, b, E:E + 1].bitcast(I32), 0),
                                        ysb[:, b % 2, :], None, compute_op=ALU.add).then_inc(s("acc_add"), 16)

        @block.scalar
        def _(act):
            for m, w in enumerate((wq, wk, wv, wo)):
                act.dma_start(w_nat[:, m], w.rearrange("(c p) d -> p c d", p=P)).then_inc(s("w_in"), 16)
            act.dma_start(gnat, gate_w).then_inc(s("gate_in"), 16)
            act.dma_start(bias_b, b_proj.unsqueeze(0).to_broadcast([P, D])).then_inc(s("bias_in"), 16)
            act.wait_ge(s("w_tr"), 1)
            for i in range(3):
                nc.scalar.activation(wprojT[:, 0, i * 512:(i + 1) * 512], bank[i][:, :], ACT.Copy,
                                     scale=WS).then_inc(s("fw_hi"), 1)

            def w_hi(m):
                act.wait_ge(s("w_tr"), m + 2 if m < 2 else 4)
                nc.scalar.activation(wT[:, 0, m], bank[3 + m][:, :], ACT.Copy, scale=WS).then_inc(s("fw_hi"), 1)

            def px_hi(T):
                act.wait_ge(s("px_tr"), T + 1)
                b = 2 * (T % 2)
                nc.scalar.activation(pxT[:, T % 2, 0, 0:512], bank[b][:, :], ACT.Copy, scale=PS).then_inc(s("px_hi"), 1)
                nc.scalar.activation(pxT[:, T % 2, 0, 512:PD], bank[b + 1][:, 0:D], ACT.Copy, scale=PS).then_inc(s("px_hi"), 1)

            def x_hi(T):
                act.wait_ge(s("x_tr"), T + 1)
                for c in range(DC):
                    ins = nc.scalar.activation(x1_at(0, c, T), bank[6 + T % 2][:, c * P:(c + 1) * P].rearrange("p (w j) -> p w j", w=2),
                                               ACT.Copy, scale=XS)
                ins.then_inc(s("x_hi"), 1)
            def std_dev(T, sfx):
                act.wait_ge(s("ag" + sfx), T + 1)
                nc.scalar.activation(std[:, T:T + 1], mv[:, T, 1:2], ACT.Sqrt, bias=eps[:, :]).then_inc(s("sd" + sfx), 1)
            act.wait_ge(s("consts"), 1)
            for m in range(4):
                w_hi(m)
            nc.scalar.copy(gateT[:, :, :].rearrange("p c e -> p (c e)"),
                           bank[7][:, 0:DC * E]).then_inc(s("gateT_s"), 1)
            px_hi(0)
            px_hi(1)
            for T in range(TILES + 1):
                if T:
                    x_hi(T - 1)
                if T < TILES:
                    std_dev(T, "")
                if T + 2 < TILES:
                    px_hi(T + 2)
                if T in (4, 5, 6, 7, 8, 9):
                    expert_hi(act, 0, T - 4)

            def v_ev(g, a):
                act.wait_ge(s("v_mm"), g + 1)
                nc.scalar.activation(vaug[0:GT, a, :, 0:HD], bank[1][0:GT, 0:D].rearrange("p (h d) -> p h d", h=HEADS),
                                     ACT.Copy, scale=1 / (XS * WS)).then_inc(s("v_ev"), 1)

            def qk_hi(g, a):
                act.wait_ge(s("qk_mm"), g + 1)
                b = bank[0][:, 0:4 * GT].rearrange("p (m q) -> p m q", m=4)
                nc.scalar.activation(qk[:, a, 0, 0:2, :], b[:, 0:2, :], ACT.Copy, scale=even[:, :])
                nc.scalar.activation(qk[:, a, 0, 2:4, :], b[:, 0:2, :], ACT.Copy, scale=odd[:, :])
                nc.scalar.activation(qk[:, a, 0, 4:6, :], b[:, 2:4, :], ACT.Copy,
                                     scale=AS / (XS * WS)).then_inc(s("qk_hi"), 1)

            def squares(g, a):
                for r in range(4):
                    act.wait_ge(s("s_mm"), 4 * g + r + 1)
                    nc.scalar.activation(probs[0:GT, a, 4 * r:4 * r + 4, :],
                                         bank[2 + r][0:GT, 0:4 * GT].rearrange("p (h q) -> p h q", h=4),
                                         ACT.Square, bias=one[0:GT, :], scale=1 / (AS * AS)).then_inc(s("sq"), 1)

            def oT_hi(g, nj):
                act.wait_ge(s("oT_mm"), g + 1)
                for c in range(DC):
                    ins = nc.scalar.activation(oT[:, 0, c, :, bass.ds(6 * g, nj)], turned_o(c, nj), ACT.Copy, scale=AS)
                ins.then_inc(s("oT_hi"), 1)

            def o_evict(g):
                act.wait_ge(s("o_mm"), g + 1)
                if not (isinstance(g, int) and g == 0):
                    act.wait_ge(s("o_turn"), g)
                nc.scalar.copy(oraw, bank[6][:, 0:4 * GT].rearrange("p (i q) -> p i q", i=4)).then_inc(s("o_raw"), 1)

            def attend(g, a, e, chunks):
                start = g if isinstance(g, int) else 2
                if start >= 1:
                    o_evict(g - 1)
                if start >= 2:
                    oT_hi(g - 2, 6)
                squares(g, a)
                for c in chunks[:1]:
                    expert_hi(act, e, c)
                if start < GROUPS - 1:
                    qk_hi(g + 1, 1 - a)
                    v_ev(g + 1, 1 - a)
                for c in chunks[1:]:
                    expert_hi(act, e, c)
            act.wait_ge(s("pad_z"), 2)
            qk_hi(0, 0)
            v_ev(0, 0)
            attend(0, 0, 0, ())
            attend(1, 1, 1, range(0, 3))
            attend(2, 0, 1, range(3, 6))
            with act.Fori(1, 4) as i:
                attend(2 * i + 1, 1, i + 1, range(0, 3))
                attend(2 * i + 2, 0, i + 1, range(3, 6))
            attend(9, 1, 5, range(0, 3))
            attend(10, 0, 5, range(3, 4))
            o_evict(GROUPS - 1)
            oT_hi(GROUPS - 2, 6)
            oT_hi(GROUPS - 1, 64 - 6 * (GROUPS - 1))
            for c in range(4, 6):
                expert_hi(act, 5, c)

            def x2_ev(T):
                act.wait_ge(s("x2_tr"), T + 1)
                if T >= 2:
                    act.wait_ge(s("lg_mm"), T - 1)
                b = bank[2 + T % 2][:, 0:D]
                nc.scalar.copy(x2f[:, T % 2].rearrange("p c q -> p (c q)"), b).then_inc(s("x2_f"), 1)
                nc.scalar.activation(x2T[:, T, 0].rearrange("p c q -> p (c q)"), b, ACT.Copy,
                                     scale=XS).then_inc(s("x2_hi"), 1)
            for T in range(TILES + 1):
                if T < TILES:
                    std_dev(T, "2")
                if T:
                    x2_ev(T - 1)
                if T % 2 == 0 and T < 8:
                    shared_hi(act, T // 2)
            act.wait_ge(s("rt"), 2)
            nc.scalar.activation(ex, ldiff, ACT.Exp).then_inc(s("ex_s"), 1)

            def g_act(T):
                act.wait_ge(s("g_mm"), T + 1)
                if T:
                    act.wait_ge(s("g_mul"), T)
                nc.scalar.activation(gate[:, 0:SHID], bank[2 * (T % 2)][:, 0:SHID], ACT.Silu,
                                     scale=1 / (XS * WS)).then_inc(s("g_act"), 1)

            def g_hi(T):
                act.wait_ge(s("g_tr"), T + 1)
                nc.scalar.activation(hidT[:, 0, 0:SHC, :].rearrange("p c q -> p (c q)"), bank[6][:, 0:SHID],
                                     ACT.Copy, scale=HS).then_inc(s("g_hi"), 1)
            def acc_init(T):
                act.wait_ge(s("y_add"), T + 1)
                for w in range(2):
                    act.dma_start(accv[T, w], hres[64 * w:64 * w + 64, T, :]).then_inc(s("acc_init"), 16)
            g_act(0)
            for T in range(TILES):
                if T + 1 < TILES:
                    g_act(T + 1)
                g_hi(T)
                if T < 6:
                    for c in (2 * T, 2 * T + 1):
                        expert_hi(act, 6 + c // 6, c % 6)
                if T >= 2:
                    acc_init(T - 2)
            acc_init(TILES - 2)
            acc_init(TILES - 1)

            def bx_hi(b):
                act.wait_ge(s("bx_tr"), b + 1)
                nc.scalar.activation(xT[:, 0].rearrange("p c q -> p (c q)"), bank[7][:, 0:D], ACT.Copy,
                                     scale=XS).then_inc(s("bx_hi"), 1)

            def silu(b):
                for i in range(2):
                    act.wait_ge(s(f"bg{i}"), b + 1)
                    nc.scalar.activation(gate[:, i * HALF:(i + 1) * HALF], bank[2 * i][:, 0:HALF], ACT.Silu,
                                         scale=1 / (XS * WS)).then_inc(s(f"ba{i}"), 1)

            def h_hi(b):
                act.wait_ge(s("bh_tr"), b + 1)
                nc.scalar.activation(hidT[:, 0, 0:4, :].rearrange("p c q -> p (c q)"), bank[4][:, :], ACT.Copy,
                                     scale=HS).then_inc(s("bh_hi"), 1)
                nc.scalar.activation(hidT[:, 0, 4, :], bank[5][:, 0:P], ACT.Copy, scale=HS)
                nc.scalar.activation(hidT[0:HLAST, 0, 5, :], bank[5][0:HLAST, P:2 * P], ACT.Copy,
                                     scale=HS).then_inc(s("bh_hi"), 1)
            bx_hi(0)
            with act.Fori(0, BLOCKS - 1) as b:
                silu(b)
                bx_hi(b + 1)
                h_hi(b)
            silu(BLOCKS - 1)
            h_hi(BLOCKS - 1)

        @block.vector
        def _(dve):
            v = nc.vector
            for i in range(7):
                dve.wait_ge(s("fw_hi"), i + 1)
                hi, lo = ((wprojT[:, h, i * 512:(i + 1) * 512] if i < 3 else wT[:, h, i - 3]) for h in range(2))
                v.scalar_tensor_tensor(lo, bank[i][:, :], WS, hi, ALU.mult, ALU.subtract).then_inc(s("fw_lo"), 1)

            def px_lo(T):
                b = 2 * (T % 2)
                for i, (c0, c1) in enumerate(((0, 512), (512, PD))):
                    dve.wait_ge(s("px_hi"), 2 * T + i + 1)
                    ins = v.scalar_tensor_tensor(pxT[:, T % 2, 1, c0:c1], bank[b + i][:, 0:c1 - c0], PS,
                                                 pxT[:, T % 2, 0, c0:c1], ALU.mult, ALU.subtract)
                ins.then_inc(s("px_lo"), 1)

            def ln_stats(T, sfx, res, mm, psum, scale):
                h = hres[:, T, :]
                dve.wait_ge(s(mm), T + 1)
                v.scalar_tensor_tensor(h, psum, scale, h, ALU.mult, ALU.add).then_inc(s(res), 1)
                dve.wait_ge(s(res), T + 1)
                v.bn_stats(stats[:, T, :], h).then_inc(s("st" + sfx), 1)
                dve.wait_ge(s("st" + sfx), T + 1)
                v.bn_aggr(mv[:, T, :], stats[:, T, :]).then_inc(s("ag" + sfx), 1)

            def ln_apply(T, sfx, xh, dst):
                dve.wait_ge(s("sd" + sfx), T + 1)
                v.reciprocal(rstd[:, T:T + 1], std[:, T:T + 1]).then_inc(s("rs" + sfx), 1)
                dve.wait_ge(s("rs" + sfx), T + 1)
                v.tensor_scalar(dst, hres[:, T, :], mv[:, T, 0:1], rstd[:, T:T + 1], ALU.subtract,
                                ALU.mult).then_inc(s(xh), 1)

            def x_lo(T):
                dve.wait_ge(s("x_hi"), T + 1)
                for c in range(DC):
                    ins = v.scalar_tensor_tensor(x1_at(1, c, T), bank[6 + T % 2][:, c * P:(c + 1) * P].rearrange("p (w j) -> p w j", w=2),
                                                 XS, x1_at(0, c, T), ALU.mult, ALU.subtract)
                ins.then_inc(s("x_lo"), 1)
            px_lo(0)
            px_lo(1)
            dve.wait_ge(s("pos_in"), 16 * 4)
            dve.wait_ge(s("bias_in"), 16)
            for T in range(TILES):
                v.tensor_tensor(hres[:, T, :], hres[:, T, :], bias_b, ALU.add).then_inc(s("pb_add"), 1)
                dve.wait_ge(s("pb_add"), T + 1)
                ln_stats(T, "", "h_res", "h_mm", bank[4 + T % 2][:, 0:D], 1 / (PS * WS))
                if T:
                    x_lo(T - 1)
                ln_apply(T, "", "xh", xh1[:, T % 3, :])
                if T + 2 < TILES:
                    px_lo(T + 2)
                if T >= 4:
                    expert_lo(dve, 0, T - 4)
            x_lo(TILES - 1)
            expert_lo(dve, 0, 5)

            def qk_lo(g, a):
                dve.wait_ge(s("qk_hi"), g + 1)
                b = bank[0][:, 0:4 * GT].rearrange("p (m q) -> p m q", m=4)
                for m, scale in enumerate((even[:, :], odd[:, :], AS / (XS * WS))):
                    ins = v.scalar_tensor_tensor(qk[:, a, 1, 2 * m:2 * m + 2, :], b[:, 2 * (m // 2):2 * (m // 2) + 2, :],
                                                 scale, qk[:, a, 0, 2 * m:2 * m + 2, :], ALU.mult, ALU.subtract)
                ins.then_inc(s("qk_lo"), 1)

            def oT_lo(g, nj):
                dve.wait_ge(s("oT_hi"), g + 1)
                for c in range(DC):
                    at = [oT[:, h, c, :, bass.ds(6 * g, nj)] for h in range(2)]
                    ins = v.scalar_tensor_tensor(at[1], turned_o(c, nj), AS, at[0], ALU.mult, ALU.subtract)
                ins.then_inc(s("oT_lo"), 1)

            def masked(g, a):
                for r in range(4):
                    dve.wait_ge(s("sq"), 4 * g + r + 1)
                    pr = probs[0:GT, a, 4 * r:4 * r + 4, :]
                    v.scalar_tensor_tensor(pr, pr, 1.0, amask[0:GT, :].unsqueeze(1).to_broadcast([GT, 4, GT]),
                                           ALU.add, ALU.mult).then_inc(s("a_rdy"), 1)

            def o_norm(g, a):
                dve.wait_ge(s("o_turn"), g + 1)
                ov = bank[7][0:GT, :].rearrange("p (h d) -> p h d", h=HEADS)
                v.tensor_scalar(zz[0:GT, a, :], ov[:, :, HD], 2 * ATT_EPS, None, ALU.add).then_inc(s("o_z"), 1)
                dve.wait_ge(s("o_z"), g + 1)
                v.reciprocal(rz[0:GT, a, :], zz[0:GT, a, :]).then_inc(s("o_r"), 1)
                dve.wait_ge(s("o_r"), g + 1)
                v.tensor_tensor(onorm[0:GT, a, :].rearrange("p (h d) -> p h d", h=HEADS), ov[:, :, 0:HD],
                                rz[0:GT, a, :].unsqueeze(2).to_broadcast([GT, HEADS, HD]), ALU.mult).then_inc(s("o_n"), 1)
            def attend(g, a, e, chunks):
                start = g if isinstance(g, int) else 2
                if start >= 2:
                    oT_lo(g - 2, 6)
                masked(g, a)
                if start >= 1:
                    o_norm(g - 1, 1 - a)
                for c in chunks[:1]:
                    expert_lo(dve, e, c)
                if start < GROUPS - 1:
                    qk_lo(g + 1, 1 - a)
                for c in chunks[1:]:
                    expert_lo(dve, e, c)
            dve.wait_ge(s("consts"), 1)
            qk_lo(0, 0)
            attend(0, 0, 0, ())
            attend(1, 1, 1, range(0, 3))
            attend(2, 0, 1, range(3, 6))
            with dve.Fori(1, 4) as i:
                attend(2 * i + 1, 1, i + 1, range(0, 3))
                attend(2 * i + 2, 0, i + 1, range(3, 6))
            attend(9, 1, 5, range(0, 3))
            attend(10, 0, 5, range(3, 4))
            oT_lo(GROUPS - 2, 6)
            o_norm(GROUPS - 1, 0)
            oT_lo(GROUPS - 1, 64 - 6 * (GROUPS - 1))

            dve.wait_ge(s("zero_done"), 64)
            dve.wait_ge(s("tok_i"), 1)
            v.tensor_scalar(tokid[64:P, :], tokid[64:P, :], 18 * 64 - 1, None, ALU.subtract).then_inc(s("tok_i"), 1)
            dve.wait_ge(s("tok_i"), 2)
            v.tensor_copy(xh2[:, :, ROW - 1].bitcast(I32), tokid[:, :])

            def x2_lo(T):
                dve.wait_ge(s("x2_hi"), T + 1)
                v.scalar_tensor_tensor(x2T[:, T, 1].rearrange("p c q -> p (c q)"), bank[2 + T % 2][:, 0:D], XS,
                                       x2T[:, T, 0].rearrange("p c q -> p (c q)"), ALU.mult,
                                       ALU.subtract).then_inc(s("x2_lo"), 1)
            for T in range(TILES):
                ln_stats(T, "2", "op_res", "op_mm", bank[OP[T % 4]][:, 0:D], 1 / (AS * WS))
                if T:
                    x2_lo(T - 1)
                if T < 2:
                    expert_lo(dve, 5, 4 + T)
                ln_apply(T, "2", "xh2_s", xh2[:, T, 0:D])
                if T % 2 == 1 and T < 8:
                    shared_lo(dve, T // 2)
            x2_lo(TILES - 1)

            n = [0]

            def step(ins):
                n[0] += 1
                ins.then_inc(s("rt"), 1)
                dve.wait_ge(s("rt"), n[0])

            def bc(col):
                return col.unsqueeze(2).to_broadcast([P, TILES, E])

            dve.wait_ge(s("lg_mm"), TILES)
            lg = bank[4][:, 0:TILES * E].rearrange("p (t e) -> p t e", e=E)
            step(v.tensor_reduce(lmax, lg, AX.X, ALU.max))
            step(v.tensor_tensor(ldiff, lg, bc(lmax), ALU.subtract))
            dve.wait_ge(s("ex_s"), 1)
            step(v.tensor_reduce(esum, ex, AX.X, ALU.add))
            step(v.reciprocal(rsum, esum))
            step(v.tensor_tensor(score, ex, bc(rsum), ALU.mult))
            step(v.tensor_reduce(w_1, score, AX.X, ALU.max))
            step(v.tensor_tensor(eq1, score, bc(w_1), ALU.is_equal))
            step(v.tensor_tensor(cand1, eq1, rank[:, :].unsqueeze(1).to_broadcast([P, TILES, E]), ALU.mult))
            step(v.tensor_reduce(best1, cand1, AX.X, ALU.max))
            step(v.tensor_tensor(sel1, cand1, bc(best1), ALU.is_equal))
            step(v.scalar_tensor_tensor(score2, sel1, -2.0, score, ALU.mult, ALU.add))
            step(v.tensor_reduce(w_2, score2, AX.X, ALU.max))
            step(v.tensor_tensor(eq2, score2, bc(w_2), ALU.is_equal))
            step(v.tensor_tensor(cand2, eq2, rank[:, :].unsqueeze(1).to_broadcast([P, TILES, E]), ALU.mult))
            step(v.tensor_reduce(best2, cand2, AX.X, ALU.max))
            step(v.tensor_tensor(sel2, cand2, bc(best2), ALU.is_equal))
            v.tensor_tensor(sel, sel1, sel2, ALU.add).then_inc(s("sel_s"), 1)
            v.tensor_tensor(xh2[:, :, D:D + E], score, sel1, ALU.mult).then_inc(s("rt"), 1)
            n[0] += 1
            dve.wait_ge(s("rt"), n[0])
            step(v.tensor_tensor(ps1, score, sel2, ALU.mult))
            step(v.tensor_tensor(xh2[:, :, D:D + E], xh2[:, :, D:D + E], ps1, ALU.add))
            v.memset(tsum[0][:, 0:8, :], 0.0)
            v.memset(tsum[1][:, 0:8, :], 0.0)
            v.memset(csum[0][:, 0:8], 0.0)
            v.memset(csum[1][:, 0:8], 0.0)
            dve.wait_ge(s("pre_mm"), 1)
            step(v.tensor_copy(tsum[0][:, 8:, :], bank[5][:, P:P + TILES * E].rearrange("p (t e) -> p t e", e=E)))
            cur = 0
            for d in (1, 2, 4, 8):
                step(v.tensor_tensor(tsum[1 - cur][:, 8:, :], tsum[cur][:, 8:, :],
                                     tsum[cur][:, 8 - d:8 - d + TILES, :], ALU.add))
                cur = 1 - cur
            incl = tsum[cur]
            step(v.tensor_tensor(cmp_n, incl[:, 7 + TILES, :].unsqueeze(2).to_broadcast([P, E, TILES]),
                                 thr[:, :].unsqueeze(1).to_broadcast([P, E, TILES]), ALU.is_gt))
            step(v.tensor_reduce(csum[0][:, 8:], cmp_n, AX.X, ALU.add))
            cc = 0
            for d in (1, 2, 4):
                step(v.tensor_tensor(csum[1 - cc][:, 8:], csum[cc][:, 8:], csum[cc][:, 8 - d:8 - d + E], ALU.add))
                cc = 1 - cc
            ends = csum[cc]
            step(v.tensor_tensor(pos, bank[5][:, 0:TILES * E].rearrange("p (t e) -> p t e", e=E),
                                 incl[:, 7:7 + TILES, :], ALU.add))
            step(v.scalar_tensor_tensor(pos, ends[:, 7:7 + E].unsqueeze(1).to_broadcast([P, TILES, E]),
                                        float(P), pos, ALU.mult, ALU.add))
            v.tensor_tensor(ps1, pos, sel1, ALU.mult)
            step(v.tensor_tensor(ps2, pos, sel2, ALU.mult))
            v.tensor_reduce(slot1f, ps1, AX.X, ALU.add)
            step(v.tensor_reduce(slot2f, ps2, AX.X, ALU.add))
            v.tensor_copy(slot[:, 0, :], slot1f)
            v.tensor_copy(slot[:, 1, :], slot2f).then_inc(s("slot_s"), 1)
            step(v.tensor_tensor(cmp_b, ends[:, 8:].unsqueeze(1).to_broadcast([P, BLOCKS, E]),
                                 bidx[:, :].unsqueeze(2).to_broadcast([P, BLOCKS, E]), ALU.is_le))
            step(v.tensor_reduce(blkf, cmp_b, AX.X, ALU.add))
            v.tensor_scalar(blk[:, :], blkf, float(E - 1), None, ALU.min).then_inc(s("blk_s"), 1)
            step(v.tensor_scalar(rblk, blkf, float(E - 1), -1.0, ALU.min, ALU.mult))
            step(v.tensor_scalar(rblk, rblk, float(E), None, ALU.add))
            step(v.tensor_tensor(onehot, rank[:, :].unsqueeze(1).to_broadcast([P, BLOCKS, E]),
                                 rblk.unsqueeze(2).to_broadcast([P, BLOCKS, E]), ALU.is_equal))

            def g_mul(T):
                dve.wait_ge(s("g_act"), T + 1)
                if T:
                    dve.wait_ge(s("g_tr"), T)
                v.scalar_tensor_tensor(hid[:, 0:SHID], bank[2 * (T % 2) + 1][:, 0:SHID], 1 / (XS * WS), gate[:, 0:SHID],
                                       ALU.mult, ALU.mult).then_inc(s("g_mul"), 1)

            def g_lo(T):
                dve.wait_ge(s("g_hi"), T + 1)
                v.scalar_tensor_tensor(hidT[:, 1, 0:SHC, :].rearrange("p c q -> p (c q)"), bank[6][:, 0:SHID], HS,
                                       hidT[:, 0, 0:SHC, :].rearrange("p c q -> p (c q)"), ALU.mult,
                                       ALU.subtract).then_inc(s("g_lo"), 1)

            def y_add(T):
                dve.wait_ge(s("y_mm"), T + 1)
                v.scalar_tensor_tensor(hres[:, T, :], bank[7][:, 0:D], 1 / (HS * WS), hres[:, T, :],
                                       ALU.mult, ALU.add).then_inc(s("y_add"), 1)
            g_mul(0)
            for T in range(TILES):
                if T + 1 < TILES:
                    g_mul(T + 1)
                g_lo(T)
                if T < 6:
                    for c in (2 * T, 2 * T + 1):
                        expert_lo(dve, 6 + c // 6, c % 6)
                if T:
                    y_add(T - 1)
            y_add(TILES - 1)

            dve.wait_ge(s("meta_in"), 16)
            step(v.tensor_tensor(erow, meta[:, :, 0:E], onehot, ALU.mult))
            step(v.tensor_reduce(wts[:, :], erow, AX.X, ALU.add))

            def mul(b):
                for i in range(2):
                    dve.wait_ge(s(f"ba{i}"), b + 1)
                    ins = v.scalar_tensor_tensor(hid[:, i * HALF:(i + 1) * HALF], bank[2 * i + 1][:, 0:HALF],
                                                 1 / (XS * WS), gate[:, i * HALF:(i + 1) * HALF], ALU.mult, ALU.mult)
                ins.then_inc(s("bm"), 1)

            def bx_lo(b):
                dve.wait_ge(s("bx_hi"), b + 1)
                v.scalar_tensor_tensor(xT[:, 1].rearrange("p c q -> p (c q)"), bank[7][:, 0:D], XS,
                                       xT[:, 0].rearrange("p c q -> p (c q)"), ALU.mult,
                                       ALU.subtract).then_inc(s("bx_lo"), 1)

            def y_ev(b, a, added):
                if added is not None:
                    dve.wait_ge(s("acc_add"), added)
                dve.wait_ge(s("by_mm"), b + 1)
                v.tensor_scalar(ysb[:, a, :], bank[6][:, 0:D], wts[:, bass.ds(b, 1)], 1 / (HS * WS),
                                ALU.mult, ALU.mult).then_inc(s("by_ev"), 1)

            def h_lo(b):
                dve.wait_ge(s("bh_hi"), 2 * b + 1)
                v.scalar_tensor_tensor(hidT[:, 1, 0:4, :].rearrange("p c q -> p (c q)"), bank[4][:, :], HS,
                                       hidT[:, 0, 0:4, :].rearrange("p c q -> p (c q)"), ALU.mult, ALU.subtract)
                dve.wait_ge(s("bh_hi"), 2 * b + 2)
                v.scalar_tensor_tensor(hidT[:, 1, 4, :], bank[5][:, 0:P], HS, hidT[:, 0, 4, :], ALU.mult, ALU.subtract)
                v.scalar_tensor_tensor(hidT[0:HLAST, 1, 5, :], bank[5][0:HLAST, P:2 * P], HS, hidT[0:HLAST, 0, 5, :],
                                       ALU.mult, ALU.subtract).then_inc(s("bh_lo"), 1)
            bx_lo(0)
            for b in range(3):
                mul(b)
                bx_lo(b + 1)
                if b:
                    y_ev(b - 1, (b - 1) % 2, None)
                h_lo(b)
            with dve.Fori(0, (BLOCKS - 5) // 2) as i:
                for a in (0, 1):
                    b = 2 * i + a + 3
                    mul(b)
                    bx_lo(b + 1)
                    y_ev(b - 1, a, 16 * (2 * i + a) + 16)
                    h_lo(b)
            for b in range(BLOCKS - 2, BLOCKS):
                mul(b)
                if b + 1 < BLOCKS:
                    bx_lo(b + 1)
                y_ev(b - 1, (b - 1) % 2, 16 * (b - 2))
                h_lo(b)
            y_ev(BLOCKS - 1, 0, 16 * (BLOCKS - 2))

        @block.tensor
        def _(pe):
            t = nc.tensor
            pe.wait_ge(s("consts"), 1)
            pe.wait_ge(s("wproj_in"), 16)
            for c in range(DC):
                for k in range(PDC):
                    ins = t.transpose(bank[k // 2][:, (k % 2) * D + c * P:(k % 2) * D + (c + 1) * P],
                                      wproj_nat[:, c, k * P:(k + 1) * P], ident[:, :])
            ins.then_inc(s("w_tr"), 1)
            for m in range(4):
                if m < 2:
                    pe.wait_ge(s("w_in"), 64)
                for c in range(DC):
                    for k in range(DC):
                        ins = t.transpose(bank[3 + m][:, k * D + c * P:k * D + (c + 1) * P],
                                          w_nat[:, m, c, k * P:(k + 1) * P], ident[:, :])
                if m < 2:
                    ins.then_inc(s("w_tr"), 1)
            pe.wait_ge(s("gate_in"), 16)
            for k in range(DC):
                ins = t.transpose(bank[7][:, k * E:(k + 1) * E], gnat[:, k * P:(k + 1) * P], ident[0:E, 0:E])
            ins.then_inc(s("w_tr"), 1)

            def passes(psum, stat, hi, lo, first, last):
                t.matmul(psum, stat(0), lo, start=first, stop=False)
                t.matmul(psum, stat(0), hi, start=False, stop=False)
                return t.matmul(psum, stat(1), hi, start=False, stop=last)

            def tr(T):
                pe.wait_ge(s(f"px_in{T % 3}"), 32 * (T // 3) + 32)
                if T < 2:
                    pe.wait_ge(s("fw_lo"), 2 * T + 2 if T == 0 else 4)
                for k in range(PDC):
                    ins = t.transpose(bank[2 * (T % 2) + k // 4][:, (k % 4) * P:(k % 4 + 1) * P],
                                      px[:, T % 3, k * P:(k + 1) * P], ident[:, :])
                ins.then_inc(s("px_tr"), 1)

            def mm(T):
                pe.wait_ge(s("px_lo"), T + 1)
                if T < 2:
                    pe.wait_ge(s("fw_lo"), 7)
                else:
                    pe.wait_ge(s("h_res"), T - 1)
                for k in range(PDC):
                    ins = passes(bank[4 + T % 2][:, 0:D], lambda h: pxT[:, T % 2, h, k * P:(k + 1) * P],
                                 wprojT[:, 0, k * D:(k + 1) * D], wprojT[:, 1, k * D:(k + 1) * D], k == 0, k == PDC - 1)
                ins.then_inc(s("h_mm"), 1)

            def xt(T):
                pe.wait_ge(s("xh"), T + 1)
                if T < 2:
                    pe.wait_ge(s("gateT_s"), 1)
                else:
                    pe.wait_ge(s("x_lo"), T - 1)
                for k in range(DC):
                    ins = t.transpose(bank[6 + T % 2][:, k * P:(k + 1) * P], xh1[:, T % 3, k * P:(k + 1) * P], ident[:, :])
                ins.then_inc(s("x_tr"), 1)
            tr(0)
            tr(1)
            for T in range(TILES):
                mm(T)
                if T + 2 < TILES:
                    tr(T + 2)
                if T:
                    xt(T - 1)
            xt(TILES - 1)
            pe.wait_ge(s("x_lo"), TILES)
            pe.wait_ge(s("pad_z"), 2)

            def project(g, a, first=False):
                x = [[x1T[:, h, k, bass.ds(g * GT, GT)] for k in range(DC)] for h in range(2)]
                for m in range(2):
                    for c in range(DC):
                        for k in range(DC):
                            at = k * D + c * P
                            ins = passes(bank[0][:, (2 * m + c) * GT:(2 * m + c + 1) * GT],
                                         lambda h: wT[:, h, m, at:at + P], x[0][k], x[1][k], k == 0, k == DC - 1)
                ins.then_inc(s("qk_mm"), 1)
                if not first:
                    pe.wait_ge(s("v_ev"), g)
                for k in range(DC):
                    ins = passes(bank[1][0:GT, 0:D], lambda h: x[h][k], wT[:, 0, 2, k * D:(k + 1) * D],
                                 wT[:, 1, 2, k * D:(k + 1) * D], k == 0, k == DC - 1)
                ins.then_inc(s("v_mm"), 1)

            def scores(g, a):
                pe.wait_ge(s("qk_lo"), g + 1)
                for r in range(4):
                    rows = slice(32 * r, 32 * r + 32)
                    for c in range(DC):
                        ins = passes(bank[2 + r][0:GT, 2 * c * GT:2 * (c + 1) * GT], lambda h: qk[rows, a, h, 4 + c, :],
                                     qk[rows, a, 0, c:c + 3:2, :], qk[rows, a, 1, c:c + 3:2, :], True, True)
                    ins.then_inc(s("s_mm"), 1)

            def values(g, a):
                if not (isinstance(g, int) and g == 0):
                    pe.wait_ge(s("o_raw"), g)
                pe.wait_ge(s("v_ev"), g + 1)
                for r in range(4):
                    pe.wait_ge(s("a_rdy"), 4 * g + r + 1)
                    for i in range(4):
                        h = 8 * (i // 2) + 2 * r + i % 2
                        n = 32 * (h % 4)
                        ins = t.matmul(bank[6][n:n + VW, h // 4 * GT:(h // 4 + 1) * GT], vaug[0:GT, a, h, :],
                                       probs[0:GT, a, 4 * r + i, :], start=True, stop=True)
                ins.then_inc(s("o_mm"), 1)

            def by_query(g, before):
                pe.wait_ge(s("o_raw"), g + 1)
                if before:
                    pe.wait_ge(s("oT_lo"), g)
                for i in range(4):
                    ins = t.transpose(bank[7][0:GT, i * P:(i + 1) * P], oraw[:, i, :], ident[:, :])
                ins.then_inc(s("o_turn"), 1)

            def turn_o(g, a):
                pe.wait_ge(s("o_n"), g + 1)
                for k in range(DC):
                    ins = t.transpose(bank[7][:, k * GT:(k + 1) * GT], onorm[0:GT, a, k * P:(k + 1) * P],
                                      ident[0:GT, 0:GT])
                ins.then_inc(s("oT_mm"), 1)

            def attend(g, a):
                start = g if isinstance(g, int) else 2
                scores(g, a)
                if start >= 1:
                    by_query(g - 1, start >= 2)
                if start < GROUPS - 1:
                    project(g + 1, 1 - a)
                values(g, a)
                if start >= 1:
                    turn_o(g - 1, 1 - a)
            project(0, 0, first=True)
            attend(0, 0)
            attend(1, 1)
            attend(2, 0)
            with pe.Fori(1, 4) as i:
                attend(2 * i + 1, 1)
                attend(2 * i + 2, 0)
            attend(9, 1)
            attend(10, 0)
            by_query(GROUPS - 1, True)
            turn_o(GROUPS - 1, 0)

            pe.wait_ge(s("oT_lo"), GROUPS)

            def oproj(T):
                if T >= 4:
                    pe.wait_ge(s("op_res"), T - 3)
                for k in range(DC):
                    ins = passes(bank[OP[T % 4]][:, 0:D], lambda h: oT[:, h, k, 2 * T:2 * T + 2, :].rearrange("p w j -> p (w j)"),
                                 wT[:, 0, 3, k * D:(k + 1) * D], wT[:, 1, 3, k * D:(k + 1) * D], k == 0, k == DC - 1)
                ins.then_inc(s("op_mm"), 1)

            def x2t(T):
                pe.wait_ge(s("xh2_s"), T + 1)
                for k in range(DC):
                    ins = t.transpose(bank[2 + T % 2][:, k * P:(k + 1) * P], xh2[:, T, k * P:(k + 1) * P], ident[:, :])
                ins.then_inc(s("x2_tr"), 1)

            def logits(T):
                pe.wait_ge(s("x2_f"), T + 1)
                for k in range(DC):
                    ins = t.matmul(bank[4][:, T * E:(T + 1) * E], x2f[:, T % 2, k, :], gateT[:, k, :],
                                   start=(k == 0), stop=(k == DC - 1))
                ins.then_inc(s("lg_mm"), 1)
            for T in range(4):
                oproj(T)
            for T in range(TILES):
                if T >= 2:
                    pe.wait_ge(s("x2_lo"), T - 1)
                x2t(T)
                if T + 4 < TILES:
                    oproj(T + 4)
                if T:
                    logits(T - 1)
            logits(TILES - 1)

            def s_up(T):
                if T >= 2:
                    pe.wait_ge(s("g_mul"), T - 1)
                for i in range(2):
                    for k in range(DC):
                        o = (i * DC + k) * SHID
                        ins = passes(bank[2 * (T % 2) + i][:, 0:SHID], lambda h: x2T[:, T, h, k, :],
                                     shared_w[:, 0, o:o + SHID], shared_w[:, 1, o:o + SHID], k == 0, k == DC - 1)
                ins.then_inc(s("g_mm"), 1)
            pe.wait_ge(s("w_lo"), 40)
            pe.wait_ge(s("x2_lo"), TILES)
            s_up(0)
            pe.wait_ge(s("sel_s"), 1)
            selr = sel.rearrange("p t e -> p (t e)")
            t.matmul(bank[5][:, 0:TILES * E], tri[:, :], selr, start=True, stop=True)
            t.matmul(bank[5][:, P:P + TILES * E], ones[:, :], selr, start=True, stop=True).then_inc(s("pre_mm"), 1)

            def s_turn(T):
                pe.wait_ge(s("g_mul"), T + 1)
                if T:
                    pe.wait_ge(s("g_lo"), T)
                for k in range(SHC):
                    ins = t.transpose(bank[6][:, k * P:(k + 1) * P], hid[:, k * P:(k + 1) * P], ident[:, :])
                ins.then_inc(s("g_tr"), 1)

            def s_down(T):
                pe.wait_ge(s("g_lo"), T + 1)
                if T:
                    pe.wait_ge(s("y_add"), T)
                for k in range(SHC):
                    o = 2 * DC * SHID + k * D
                    ins = passes(bank[7][:, 0:D], lambda h: hidT[:, h, k, :], shared_w[:, 0, o:o + D],
                                 shared_w[:, 1, o:o + D], k == 0, k == SHC - 1)
                ins.then_inc(s("y_mm"), 1)
            for T in range(TILES):
                if T + 1 < TILES:
                    s_up(T + 1)
                if T:
                    s_down(T - 1)
                s_turn(T)
            s_down(TILES - 1)

            pe.wait_ge(s("y_add"), TILES)
            pe.wait_ge(s("blk_s"), 1)
            pe.wait_ge(s("w_lo"), 52)

            def bx(b, a, count):
                pe.wait_ge(s(f"x_in{a}"), count)
                for k in range(DC):
                    ins = t.transpose(bank[7][:, k * P:(k + 1) * P], xblk[:, a, k * P:(k + 1) * P], ident[:, :])
                ins.then_inc(s("bx_tr"), 1)

            def expert_of(b):
                return pe.value_load(blk[0:1, bass.ds(b, 1)], min_val=0, max_val=E - 1)

            def up(b):
                e = expert_of(b)
                pe.wait_ge(s("bx_lo"), b + 1)
                for i in range(2):
                    for j, base in enumerate((W1, W3)):
                        for k in range(DC):
                            o = base + k * HID + i * HALF
                            ins = passes(bank[2 * i + j][:, 0:HALF], lambda h: xT[:, h, k, :],
                                         expert_at(e, 0, o, HALF), expert_at(e, 1, o, HALF), k == 0, k == DC - 1)
                    ins.then_inc(s(f"bg{i}"), 1)

            def bturn(b):
                pe.wait_ge(s("bm"), b + 1)
                for k in range(HC):
                    m = P if k < HC - 1 else HLAST
                    ins = t.transpose(bank[4 + k // 4][0:m, (k % 4) * P:(k % 4 + 1) * P], hid[:, k * P:k * P + m],
                                      ident[:, :])
                ins.then_inc(s("bh_tr"), 1)

            def down(b):
                e = expert_of(b)
                pe.wait_ge(s("bh_lo"), b + 1)
                for k in range(HC):
                    m = P if k < HC - 1 else HLAST
                    o = W2 + k * D
                    ins = passes(bank[6][:, 0:D], lambda h: hidT[0:m, h, k, :], expert_at(e, 0, o, D)[0:m],
                                 expert_at(e, 1, o, D)[0:m], k == 0, k == HC - 1)
                ins.then_inc(s("by_mm"), 1)
            bx(0, 0, 16)
            up(0)
            bx(1, 1, 16)
            bturn(0)
            with pe.Fori(0, (BLOCKS - 3) // 2) as i:
                for a in (0, 1):
                    b = 2 * i + a + 1
                    up(b)
                    bx(b + 1, a, 16 * i + 32)
                    down(b - 1)
                    bturn(b)
            up(BLOCKS - 2)
            bx(BLOCKS - 1, 0, 16 * ((BLOCKS + 1) // 2))
            down(BLOCKS - 3)
            bturn(BLOCKS - 2)
            up(BLOCKS - 1)
            down(BLOCKS - 2)
            bturn(BLOCKS - 1)
            down(BLOCKS - 1)


_INS = ["x", "L0_tok_W_proj", "L0_tok_b_proj", "L0_tok_pos_emb", "L0_attn_Wq", "L0_attn_Wk", "L0_attn_Wv", "L0_attn_Wo",
        "L0_ffn_gate_w", "L0_ffn_w1", "L0_ffn_w2", "L0_ffn_w3", "L0_ffn_sw1", "L0_ffn_sw2", "L0_ffn_sw3"]


def kernel(**inputs):
    import numpy as np
    import concourse.bacc as bacc
    from concourse.bass_utils import run_bass_kernel_spmd

    nc = bacc.Bacc("TRN2", target_bir_lowering=False, num_devices=1)
    arrays, args = {}, []
    for name in _INS:
        a = np.ascontiguousarray(inputs[name])
        arrays[f"in_{name}"] = a
        args.append(nc.dram_tensor(f"in_{name}", a.shape, mybir.dt.from_np(a.dtype), kind="ExternalInput").ap())
    args.append(nc.dram_tensor("out_0", (IMAGES, SEQ, D), F32, kind="ExternalOutput").ap())
    vit_moe(nc, *args)
    r = run_bass_kernel_spmd(nc, [arrays], core_ids=[0])
    return r.results[0]["out_0"]
```

```python
from contextlib import ExitStack

import concourse.bass as bass
from concourse import mybir

F32 = mybir.dt.float32
F16 = mybir.dt.float16
I32 = mybir.dt.int32
ALU = mybir.AluOpType
ACT = mybir.ActivationFunctionType
AX = mybir.AxisListType

P = 128
IMAGES, SIDE, CH, PATCH = 32, 96, 3, 16
PER_SIDE = SIDE // PATCH
SEQ = PER_SIDE * PER_SIDE
TOK = IMAGES * SEQ
D = 256
DC = D // P
PD = PATCH * PATCH * CH
PDC = PD // P
RUN = PATCH * CH
TILES = TOK // P
HEADS, HD = 16, 16
VW = 32
GIMG = 3
GT = GIMG * SEQ
GROUPS = -(-IMAGES // GIMG)
GPAD = GROUPS * GT
E, HID, SHID = 8, 704, 384
HALF = HID // 2
HC = -(-HID // P)
HLAST = HID - (HC - 1) * P
SHC = SHID // P
BLOCKS = (2 * TOK + E * (P - 1)) // P
SLOTS = BLOCKS * P
W1, W3, W2, WEXP = 0, DC * HID, 2 * DC * HID, 2 * DC * HID + HC * D
ROW = D + E + 1
SW = 2 * DC * SHID + SHC * D
STAGE = 3 * D
LATE_CHUNKS = ((), (0,), (1, 2), (3, 4), (5, 6), (7, 8), (9, 10), (11,), ())
WS, XS, HS = 256.0, 256.0, 16.0
PS, AS = 64.0, 64.0
QSCALE = HD ** -0.5 * AS / (XS * WS)
LN_EPS = 1e-5
ATT_EPS = 1e-6


def vit_moe(nc, x, w_proj, b_proj, pos_emb, wq, wk, wv, wo, gate_w, w1, w2, w3, sw1, sw2, sw3, out):
    ctx = ExitStack()
    with ctx:
        def sb(name, shape, dt=F32):
            return ctx.enter_context(nc.sbuf_tensor(name, shape, dt))

        def sem(name):
            return ctx.enter_context(nc.semaphore(name))

        slots_x = nc.dram_tensor("slots_x", [SLOTS, ROW], F32, kind="Internal").ap()
        acc = nc.dram_tensor("acc", [TOK + P, D], F32, kind="Internal").ap()

        experts = sb("experts", [P, E * 2 * WEXP], F16)
        early = experts[:, 6 * 2 * WEXP:].bitcast(F32)
        stage = sb("stage", [P, 2, STAGE])
        px = early[:, 0:3 * PD].rearrange("p (s d) -> p s d", s=3)
        probs = early[:, 0:2 * HEADS * GT].rearrange("p (a h q) -> p a h q", a=2, h=HEADS)
        o = 2 * HEADS * GT
        wproj_nat = early[:, o:o + DC * PD].rearrange("p (c d) -> p c d", c=DC)
        qk = early[:, o:o + 2 * 6 * GT].bitcast(F16).rearrange("p (a h m q) -> p a h m q", a=2, h=2, m=6)
        o += DC * PD
        w_nat = early[:, o:o + 4 * DC * D].rearrange("p (m c d) -> p m c d", m=4, c=DC)
        oraw = early[:, o:o + 4 * GT].rearrange("p (i q) -> p i q", i=4)
        o += 4 * DC * D
        vaug = early[:, o:o + 2 * HEADS * VW].rearrange("p (a h d) -> p a h d", a=2, h=HEADS)
        o += 2 * HEADS * VW
        onorm = early[:, o:o + 2 * D].rearrange("p (a d) -> p a d", a=2)
        o += 2 * D
        shared_w = sb("shared_w", [P, 2, SW], F16)
        xa = sb("xa", [P, DC * GPAD])
        x1T = xa[:, :].bitcast(F16).rearrange("p (h c t) -> p h c t", h=2, c=DC)
        x2T = xa[:, 0:TILES * D].bitcast(F16).rearrange("p (t h c q) -> p t h c q", t=TILES, h=2, c=DC)
        hres = sb("hres", [P, TILES, D])
        xh2 = sb("xh2", [P, TILES, ROW])
        ob = sb("ob", [P, 3 * PD])
        pxT = ob[:, 0:2 * PD].bitcast(F16).rearrange("p (s h q) -> p s h q", s=2, h=2)
        oT = ob[:, :].bitcast(F16).rearrange("p (h c t j) -> p h c t j", h=2, c=DC, t=2 * TILES)
        fw = sb("fw", [P, PDC * D + 4 * DC * D])
        wprojT = fw[:, 0:PDC * D].bitcast(F16).rearrange("p (h q) -> p h q", h=2)
        wT = fw[:, PDC * D:].bitcast(F16).rearrange("p (h m q) -> p h m q", h=2, m=4)
        o = 0
        x2f = fw[:, o:o + 2 * D].rearrange("p (a c q) -> p a c q", a=2, c=DC)
        xblk = fw[:, o:o + 2 * D].rearrange("p (a d) -> p a d", a=2); o += 2 * D
        xT = fw[:, o:o + D].bitcast(F16).rearrange("p (h c q) -> p h c q", h=2, c=DC); o += D
        gate = fw[:, o:o + HID]; o += HID
        hid = fw[:, o:o + HID]; o += HID
        hidT = fw[:, o:o + HC * P].bitcast(F16).rearrange("p (h c q) -> p h c q", h=2, c=HC); o += HC * P
        shid = hidT.rearrange("p h c q -> p (h c q)")[:, 0:2 * SHC * P].rearrange("p (h c q) -> p h c q", h=2, c=SHC)
        ysb = fw[:, o:o + 2 * D].rearrange("p (a d) -> p a d", a=2); o += 2 * D
        assert o <= PDC * D + 4 * DC * D
        free = 3 * PD
        xh1 = early[:, free:free + 3 * D].rearrange("p (s d) -> p s d", s=3)
        bias_b = early[:, free + 3 * D:free + 4 * D]
        stage_early = xh2[:, TILES - 3:, :].rearrange("p t r -> p (t r)")[:, 0:STAGE]
        stage_late = fw[:, o - 2 * D - HC * P // 2:o - 2 * D - HC * P // 2 + STAGE]
        assert 3 * ROW >= STAGE and o - 2 * D - HC * P // 2 >= PDC * D + 4 * D
        assert o - 2 * D - HC * P // 2 + STAGE <= PDC * D + 7 * D
        ident = sb("ident", [P, P])
        tri = sb("tri", [P, P])
        ones = sb("ones", [P, P])
        amask = sb("amask", [P, GT])
        gnat = xh2[0:E, 0, 0:D]
        gateT = sb("gateT", [P, DC, E])
        even = sb("even", [P, 1])
        odd = sb("odd", [P, 1])
        one = sb("one", [P, 1])
        eps = sb("eps", [P, 1])
        stats = sb("stats", [P, TILES, 6])
        mv = sb("mv", [P, TILES, 2])
        std = sb("std", [P, TILES])
        rstd = sb("rstd", [P, TILES])
        rz = sb("rz", [P, 2, HEADS])
        zz = sb("zz", [P, 2, HEADS])
        small = [0]

        def over(n):
            v = ob[:, small[0]:small[0] + n]
            small[0] += n
            assert small[0] <= 3 * PD
            return v

        def te(n=TILES):
            return over(n * E).rearrange("p (t e) -> p t e", e=E)
        rank = sb("rank", [P, E])
        thr = sb("thr", [P, TILES])
        bidx = sb("bidx", [P, BLOCKS])
        tokid = sb("tokid", [P, TILES], I32)
        ldiff, ex, score, eq1, cand1, sel1, score2, eq2, cand2, sel2, sel = [te() for _ in range(11)]
        pos, ps1, ps2 = te(), te(), te()
        tsum = [te(8 + TILES), te(8 + TILES)]
        cmp_n = over(E * TILES).rearrange("p (e t) -> p e t", e=E)
        cmp_b = over(BLOCKS * E).rearrange("p (b e) -> p b e", e=E)
        csum = [over(8 + E), over(8 + E)]
        lmax, esum, rsum, best1, best2, w_1, w_2, slot1f, slot2f = [over(TILES) for _ in range(9)]
        blkf = over(BLOCKS)
        erow = over(BLOCKS * E).rearrange("p (b e) -> p b e", e=E)
        rblk = over(BLOCKS)
        onehot = over(BLOCKS * E).rearrange("p (b e) -> p b e", e=E)
        meta = sb("meta", [P, BLOCKS, E + 1])
        wts = sb("wts", [P, BLOCKS])
        slot = sb("slot", [P, 2, TILES], I32)
        blk = sb("blk", [P, BLOCKS], I32)

        bank = [ctx.enter_context(nc.psum_tensor(f"bank{i}", [P, 512], F32)) for i in range(8)]

        OP = (0, 1, 5, 6)

        S = {}

        def s(name):
            if name not in S:
                S[name] = sem(name)
            return S[name]

        for n in ("wproj_in w_in gate_in bias_in pos_in px_in0 px_in1 px_in2 stage_in0 stage_in1 stage_in2 w_hi w_lo zero_done "
                  "pool_step ident_s consts w_tr fw_hi fw_lo gateT_s px_tr px_hi px_lo h_mm h_res st ag sd rs xh x_tr x_hi x_lo "
                  "qk_mm qk_hi qk_lo v_mm v_ev s_mm sq a_rdy o_mm o_raw o_turn o_z o_r o_n oT_mm oT_hi oT_lo pad_z "
                  "op_mm op_res st2 ag2 sd2 rs2 xh2_s x2_tr x2_f x2_hi x2_lo lg_mm rt ex_s pre_mm sel_s slot_s blk_s "
                  "g_mm g_act g_mul g_tr g_hi g_lo y_mm y_add scat x_in0 x_in1 bx_tr bx_hi bx_lo bg0 bg1 ba0 ba1 bm meta_in "
                  "stage_z tok_i bh_tr bh_hi bh_lo by_mm by_ev acc_init acc_add out_s pb_add").split():
            s(n)

        xv = x.rearrange("b (hp ph) w c -> (b hp) ph (w c)", ph=PATCH).rearrange("(j g) ph q -> g j ph q", g=3)
        outv = out.rearrange("b s d -> (b s) d")
        accv = acc[0:TOK, :].rearrange("(j t w) d -> t w j d", t=TILES, w=2)

        block = ctx.enter_context(nc.Block())

        def load_patches(eng, G, W):
            for w in range(2):
                c = (2 * W + w) * RUN
                eng.dma_start(px[64 * w:64 * w + 64, W, :].rearrange("p (a r) -> p a r", a=PATCH),
                              xv[G, :, :, c:c + RUN]).then_inc(s(f"px_in{W}"), 16)

        def expert_chunk(e, c):
            if c < 4:
                w, k = (w1, w3)[c // 2], c % 2
                return c * HID, HID, [(P, 1, 0, HID, w[bass.ds(e, 1), k * P:(k + 1) * P, :].rearrange("e p n -> p e n"))]
            rows = w2[bass.ds(e, 1)]
            if c == 4:
                return W2, 3 * D, [(P, 3, 0, 3 * D, rows[:, 0:3 * P, :].rearrange("e (k p) n -> p (e k) n", p=P))]
            return W2 + 3 * D, 3 * D, [
                (P, 2, 0, 2 * D, rows[:, 3 * P:5 * P, :].rearrange("e (k p) n -> p (e k) n", p=P)),
                (HLAST, 1, 2 * D, 3 * D, rows[:, 5 * P:HID, :].rearrange("e p n -> p e n"))]

        def shared_chunk(c):
            if c < 2:
                return c * DC * SHID, DC * SHID, [(P, DC, 0, DC * SHID, (sw1, sw3)[c].rearrange("(k p) n -> p k n", p=P))]
            k0, k1 = ((0, 2), (2, 3))[c - 2]
            return (2 * DC * SHID + k0 * D, (k1 - k0) * D,
                    [(P, k1 - k0, 0, (k1 - k0) * D, sw2[k0 * P:k1 * P, :].rearrange("(k p) n -> p k n", p=P))])

        def arrived(e, c):
            late = (32, 16, 16)[c % 3] if isinstance(e, int) and e >= 6 else 0
            return e * 32 + c // 3 * 16 + 16 + late if c % 3 < 2 else e * 48 + c // 3 * 32 + 16 + late

        def staged(c, late):
            return (stage[:, 0], stage[:, 1], stage_late if late else stage_early)[c % 3]

        def is_late(e):
            return isinstance(e, int) and e >= 6

        def load_chunk(eng, c, late, pieces, split):
            if split is not None:
                eng.wait_ge(s("w_lo"), split)
            for parts, k, lo, hi, src in pieces:
                eng.dma_start(staged(c, late)[0:parts, lo:hi].rearrange("p (k n) -> p k n", k=k),
                              src).then_inc(s(f"stage_in{c % 3}"), 16)

        def load_expert_chunk(eng, e, c):
            split = e * 6 + c - 2 + (4 if is_late(e) else 0)
            if isinstance(e, int) and e == 0 and c < 3:
                split = None
            elif isinstance(e, int) and e == 6 and c < 3:
                split = (40, 38, 39)[c]
            load_chunk(eng, c, is_late(e), expert_chunk(e, c)[2], split)

        def split_hi(act, dst, size, c, late, count):
            act.wait_ge(s(f"stage_in{c % 3}"), count)
            nc.scalar.activation(dst, staged(c, late)[:, 0:size], ACT.Copy, scale=WS).then_inc(s("w_hi"), 1)

        def split_lo(dve, dst, hi, size, c, late, n):
            dve.wait_ge(s("w_hi"), n + 1)
            nc.vector.scalar_tensor_tensor(dst, staged(c, late)[:, 0:size], WS, hi, ALU.mult, ALU.subtract).then_inc(s("w_lo"), 1)

        def expert_at(e, half, off, size):
            return experts[:, bass.ds(e * (2 * WEXP) + (half * WEXP + off), size)]

        def expert_hi(act, e, c):
            off, size, _ = expert_chunk(e, c)
            split_hi(act, expert_at(e, 0, off, size), size, c, is_late(e), arrived(e, c))

        def expert_lo(dve, e, c):
            off, size, _ = expert_chunk(e, c)
            split_lo(dve, expert_at(e, 1, off, size), expert_at(e, 0, off, size), size, c, is_late(e),
                     e * 6 + c + (4 if is_late(e) else 0))

        def shared_hi(act, c):
            off, size, _ = shared_chunk(c)
            split_hi(act, shared_w[:, 0, off:off + size], size, c, True,
                     (6 * 48 if c % 3 == 2 else 6 * 32) + 16 * (c // 3) + 16)

        def shared_lo(dve, c):
            off, size, _ = shared_chunk(c)
            split_lo(dve, shared_w[:, 1, off:off + size], shared_w[:, 0, off:off + size], size, c, True, 36 + c)

        def x1_at(half, c, T):
            return x1T[:, half, c, 0:TOK].rearrange("p (j t w) -> p t w j", t=TILES, w=2)[:, T]

        def turned_o(c, nj):
            return bank[7][:, c * GT:(c + 1) * GT].rearrange("p (j q) -> p q j", j=6)[:, :, 0:nj]

        @block.sync
        def _(sp):
            for W in range(3):
                load_patches(sp, 0, W)
            for T in range(3, TILES):
                sp.wait_ge(s("px_tr"), T - 2)
                load_patches(sp, T // 3, T % 3)
            sp.wait_ge(s("stage_z"), 1)
            for c in range(6):
                load_expert_chunk(sp, 0, c)
            with sp.Fori(1, 5) as e:
                for c in range(6):
                    load_expert_chunk(sp, e, c)
            for c in range(6):
                load_expert_chunk(sp, 5, c)
            for c in range(4):
                if c == 2:
                    sp.wait_ge(s("v_mm"), GROUPS)
                load_chunk(sp, c, True, shared_chunk(c)[2], 34 + c)
            for e in range(6, 8):
                for c in range(6):
                    load_expert_chunk(sp, e, c)
            sp.wait_ge(s("scat"), 16 * 2 * TILES)
            sp.dma_start(meta[:, :, :], slots_x.rearrange("(b p) d -> p b d", p=P)[:, :, D:ROW]).then_inc(s("meta_in"), 16)

            def load(b, a):
                sp.dma_start(xblk[:, a, :], slots_x[bass.ds(b * P, P), 0:D]).then_inc(s(f"x_in{a}"), 16)
            load(0, 0)
            load(1, 1)
            with sp.Fori(0, (BLOCKS - 3) // 2) as i:
                for a in (0, 1):
                    sp.wait_ge(s("bx_tr"), 2 * i + a + 1)
                    load(2 * i + a + 2, a)
            sp.wait_ge(s("bx_tr"), BLOCKS - 2)
            load(BLOCKS - 1, 0)
            sp.wait_ge(s("acc_add"), 16 * BLOCKS)
            sp.dma_start(outv, acc[0:TOK, :]).then_inc(s("out_s"), 16)
            sp.wait_ge(s("out_s"), 16)

        @block.gpsimd
        def _(pool):
            n = [0]

            def step(ins):
                n[0] += 1
                ins.then_inc(s("pool_step"), 1)
                pool.wait_ge(s("pool_step"), n[0])
            step(nc.gpsimd.memset(ident[:, :], 0.0))
            nc.gpsimd.affine_select(out=ident[:, :], in_=ident[:, :], compare_op=ALU.not_equal, fill=1.0,
                                    base=0, pattern=[[-1, P]], channel_multiplier=1).then_inc(s("ident_s"), 1)
            for w in range(2):
                for b in range(2):
                    pool.dma_start(hres[64 * w + b:64 * w + 64:2, :, :],
                                   pos_emb[18 * b + w:18 * b + 18:2, :].unsqueeze(0).to_broadcast([32, TILES, D])
                                   ).then_inc(s("pos_in"), 16)
            nc.gpsimd.memset(tri[:, :], 1.0)
            nc.gpsimd.memset(ones[:, :], 1.0)
            nc.gpsimd.memset(one[:, :], 1.0)
            nc.gpsimd.memset(eps[:, :], LN_EPS)
            nc.gpsimd.memset(even[:, :], 0.0)
            nc.gpsimd.memset(odd[:, :], QSCALE)
            step(nc.gpsimd.memset(amask[:, :], 1.0))
            step(nc.gpsimd.affine_select(out=tri[:, :], in_=tri[:, :], compare_op=ALU.is_gt, fill=0.0,
                                         base=0, pattern=[[1, P]], channel_multiplier=-1))
            for r in range(4):
                step(nc.gpsimd.memset(even[32 * r:32 * r + HD, :], QSCALE))
                step(nc.gpsimd.memset(odd[32 * r:32 * r + HD, :], 0.0))
            step(nc.gpsimd.affine_select(out=amask[0:GT, :], in_=amask[0:GT, :], compare_op=ALU.is_ge, fill=0.0,
                                         base=0, pattern=[[1, GT]], channel_multiplier=-1))
            nc.gpsimd.affine_select(out=amask[0:GT, :].rearrange("p (i q) -> p i q", i=GIMG),
                                    in_=amask[0:GT, :].rearrange("p (i q) -> p i q", i=GIMG),
                                    compare_op=ALU.is_ge, fill=0.0, base=0,
                                    pattern=[[-SEQ, GIMG], [0, SEQ]], channel_multiplier=1).then_inc(s("consts"), 1)
            pool.wait_ge(s("consts"), 1)
            nc.gpsimd.memset(stage_early[HLAST:P, 2 * D:], 0.0).then_inc(s("stage_z"), 1)
            pool.wait_ge(s("stage_z"), 1)
            nc.gpsimd.memset(x1T[:, :, :, TOK:GPAD], 0.0).then_inc(s("pad_z"), 1)
            step(nc.gpsimd.memset(vaug[:, :, :, HD:VW], 0.0))
            nc.gpsimd.memset(vaug[:, :, :, HD:HD + 1], 1.0).then_inc(s("pad_z"), 1)
            for e in range(E):
                nc.gpsimd.memset(rank[:, e:e + 1], float(E - e))
            for t in range(TILES):
                nc.gpsimd.memset(thr[:, t:t + 1], float(P * t))
            for b in range(BLOCKS):
                nc.gpsimd.memset(bidx[:, b:b + 1], float(b))
            nc.gpsimd.iota(tokid[:, :], pattern=[[2, TILES]], base=0, channel_multiplier=18).then_inc(s("tok_i"), 1)
            pool.wait_ge(s("pos_in"), 16 * 4)
            pool.wait_ge(s("bias_in"), 16)
            for T in range(0, TILES, 3):
                nc.gpsimd.tensor_tensor(hres[:, T:T + 3, :], hres[:, T:T + 3, :],
                                        bias_b.unsqueeze(1).to_broadcast([P, 3, D]), ALU.add).then_inc(s("pb_add"), 1)
            pool.wait_ge(s("w_tr"), 6)
            step(nc.gpsimd.memset(xh2[:, 0:3, :], 0.0))
            step(nc.gpsimd.iota(xh2[:, 0:3, ROW - 1:ROW].bitcast(I32), pattern=[[0, 3], [0, 1]], base=TOK,
                                channel_multiplier=1))
            sv = slots_x.rearrange("(n p) d -> p n d", p=P)
            for i, a in enumerate(range(0, BLOCKS, 3)):
                k = min(3, BLOCKS - a)
                pool.wait_ge(s("s_mm"), 4 * (i + 1))
                pool.dma_start(sv[:, a:a + k, :], xh2[:, 0:k, :]).then_inc(s("zero_done"), 16)
            pool.dma_start(acc[TOK:TOK + P, :], xh2[:, 0, 0:D]).then_inc(s("zero_done"), 16)

            pool.wait_ge(s("slot_s"), 1)
            pool.wait_ge(s("zero_done"), 16 * (-(-BLOCKS // 3) + 1))
            for T in range(TILES):
                for k in range(2):
                    pool.indirect_dma_start(slots_x, bass.IndirectOffsetOnAxis(slot[:, k, T:T + 1], 0),
                                            xh2[:, T, :], None).then_inc(s("scat"), 16)
            pool.wait_ge(s("acc_init"), 32 * TILES)
            pool.wait_ge(s("meta_in"), 16)
            for b in range(BLOCKS):
                if b:
                    pool.wait_ge(s("acc_add"), 16 * b)
                pool.wait_ge(s("by_ev"), b + 1)
                pool.indirect_dma_start(acc, bass.IndirectOffsetOnAxis(meta[:, b, E:E + 1].bitcast(I32), 0),
                                        ysb[:, b % 2, :], None, compute_op=ALU.add).then_inc(s("acc_add"), 16)

        @block.scalar
        def _(act):
            act.dma_start(wproj_nat, w_proj.rearrange("(c p) d -> p c d", p=P)).then_inc(s("wproj_in"), 16)
            act.dma_start(bias_b, b_proj.unsqueeze(0).to_broadcast([P, D])).then_inc(s("bias_in"), 16)
            for m, w in enumerate((wq, wk, wv, wo)):
                act.dma_start(w_nat[:, m], w.rearrange("(c p) d -> p c d", p=P)).then_inc(s("w_in"), 16)
            act.dma_start(gnat, gate_w).then_inc(s("gate_in"), 16)
            act.wait_ge(s("w_tr"), 1)
            for i in range(3):
                nc.scalar.activation(wprojT[:, 0, i * 512:(i + 1) * 512], bank[4 + i][:, :], ACT.Copy,
                                     scale=WS).then_inc(s("fw_hi"), 1)

            def w_hi(m):
                act.wait_ge(s("w_tr"), m + 2)
                nc.scalar.activation(wT[:, 0, m], bank[7][:, :], ACT.Copy, scale=WS).then_inc(s("fw_hi"), 1)

            def px_hi(T):
                act.wait_ge(s("px_tr"), T + 1)
                b = 2 * (T % 2)
                nc.scalar.activation(pxT[:, T % 2, 0, 0:512], bank[b][:, :], ACT.Copy, scale=PS).then_inc(s("px_hi"), 1)
                nc.scalar.activation(pxT[:, T % 2, 0, 512:PD], bank[b + 1][:, 0:D], ACT.Copy, scale=PS).then_inc(s("px_hi"), 1)

            def x_hi(T):
                act.wait_ge(s("x_tr"), T + 1)
                for c in range(DC):
                    ins = nc.scalar.activation(x1_at(0, c, T), bank[6][:, c * P:(c + 1) * P].rearrange("p (w j) -> p w j", w=2),
                                               ACT.Copy, scale=XS)
                ins.then_inc(s("x_hi"), 1)
            def std_dev(T, sfx):
                act.wait_ge(s("ag" + sfx), T + 1)
                nc.scalar.activation(std[:, T:T + 1], mv[:, T, 1:2], ACT.Sqrt, bias=eps[:, :]).then_inc(s("sd" + sfx), 1)
            px_hi(0)
            px_hi(1)
            act.wait_ge(s("consts"), 1)
            std_dev(0, "")
            for T in range(TILES + 1):
                if T + 2 < TILES:
                    px_hi(T + 2)
                if T:
                    x_hi(T - 1)
                if T < 4:
                    w_hi(T)
                elif T == 5:
                    act.wait_ge(s("w_tr"), 6)
                    nc.scalar.copy(gateT[:, :, :].rearrange("p c e -> p (c e)"), bank[7][:, 0:DC * E]).then_inc(s("gateT_s"), 1)
                if T + 1 < TILES:
                    std_dev(T + 1, "")

            def v_ev(g, a):
                act.wait_ge(s("v_mm"), g + 1)
                nc.scalar.activation(vaug[0:GT, a, :, 0:HD], bank[1][0:GT, 0:D].rearrange("p (h d) -> p h d", h=HEADS),
                                     ACT.Copy, scale=1 / (XS * WS)).then_inc(s("v_ev"), 1)

            def qk_hi(g, a):
                act.wait_ge(s("qk_mm"), g + 1)
                b = bank[0][:, 0:4 * GT].rearrange("p (m q) -> p m q", m=4)
                nc.scalar.activation(qk[:, a, 0, 0:2, :], b[:, 0:2, :], ACT.Copy, scale=even[:, :])
                nc.scalar.activation(qk[:, a, 0, 2:4, :], b[:, 0:2, :], ACT.Copy, scale=odd[:, :])
                nc.scalar.activation(qk[:, a, 0, 4:6, :], b[:, 2:4, :], ACT.Copy,
                                     scale=AS / (XS * WS)).then_inc(s("qk_hi"), 1)

            def squares(g, a):
                for r in range(4):
                    act.wait_ge(s("s_mm"), 4 * g + r + 1)
                    nc.scalar.activation(probs[0:GT, a, 4 * r:4 * r + 4, :],
                                         bank[2 + r][0:GT, 0:4 * GT].rearrange("p (h q) -> p h q", h=4),
                                         ACT.Square, bias=one[0:GT, :], scale=1 / (AS * AS)).then_inc(s("sq"), 1)

            def oT_hi(g, nj):
                act.wait_ge(s("oT_mm"), g + 1)
                for c in range(DC):
                    ins = nc.scalar.activation(oT[:, 0, c, :, bass.ds(6 * g, nj)], turned_o(c, nj), ACT.Copy, scale=AS)
                ins.then_inc(s("oT_hi"), 1)

            def o_evict(g):
                act.wait_ge(s("o_mm"), g + 1)
                if not (isinstance(g, int) and g == 0):
                    act.wait_ge(s("o_turn"), g)
                nc.scalar.copy(oraw, bank[6][:, 0:4 * GT].rearrange("p (i q) -> p i q", i=4)).then_inc(s("o_raw"), 1)

            def attend(g, a, e, chunks):
                start = g if isinstance(g, int) else 2
                for c in chunks[:1]:
                    expert_hi(act, e, c)
                if start >= 1:
                    o_evict(g - 1)
                if start >= 2:
                    oT_hi(g - 2, 6)
                squares(g, a)
                for c in chunks[1:2]:
                    expert_hi(act, e, c)
                if start < GROUPS - 1:
                    qk_hi(g + 1, 1 - a)
                    v_ev(g + 1, 1 - a)
                for c in chunks[2:]:
                    expert_hi(act, e, c)
            for c in range(2):
                expert_hi(act, 0, c)
            act.wait_ge(s("pad_z"), 2)
            qk_hi(0, 0)
            v_ev(0, 0)
            attend(0, 0, 0, range(2, 6))
            attend(1, 1, 1, range(0, 3))
            attend(2, 0, 1, range(3, 6))
            with act.Fori(1, 4) as i:
                attend(2 * i + 1, 1, i + 1, range(0, 3))
                attend(2 * i + 2, 0, i + 1, range(3, 6))
            attend(9, 1, 5, range(0, 3))
            attend(10, 0, 5, range(3, 4))
            o_evict(GROUPS - 1)
            oT_hi(GROUPS - 2, 6)
            oT_hi(GROUPS - 1, 64 - 6 * (GROUPS - 1))
            for c in range(4, 6):
                expert_hi(act, 5, c)

            def x2_ev(T):
                act.wait_ge(s("x2_tr"), T + 1)
                if T >= 2:
                    act.wait_ge(s("lg_mm"), T - 1)
                b = bank[2 + T % 2][:, 0:D]
                nc.scalar.copy(x2f[:, T % 2].rearrange("p c q -> p (c q)"), b).then_inc(s("x2_f"), 1)
                nc.scalar.activation(x2T[:, T, 0].rearrange("p c q -> p (c q)"), b, ACT.Copy,
                                     scale=XS).then_inc(s("x2_hi"), 1)
            std_dev(0, "2")
            for T in range(TILES + 1):
                if T:
                    x2_ev(T - 1)
                if T % 2 == 0 and T < 8:
                    shared_hi(act, T // 2)
                if T + 1 < TILES:
                    std_dev(T + 1, "2")
            act.wait_ge(s("rt"), 2)
            nc.scalar.activation(ex, ldiff, ACT.Exp).then_inc(s("ex_s"), 1)

            def g_act(T):
                act.wait_ge(s("g_mm"), T + 1)
                if T:
                    act.wait_ge(s("g_mul"), T)
                nc.scalar.activation(gate[:, 0:SHID], bank[2 * (T % 2)][:, 0:SHID], ACT.Silu,
                                     scale=1 / (XS * WS)).then_inc(s("g_act"), 1)

            def g_hi(T):
                act.wait_ge(s("g_tr"), T + 1)
                nc.scalar.activation(shid[:, 0].rearrange("p c q -> p (c q)"), bank[6][:, 0:SHID],
                                     ACT.Copy, scale=HS).then_inc(s("g_hi"), 1)
            def acc_init(T):
                act.wait_ge(s("y_add"), T + 1)
                for w in range(2):
                    act.dma_start(accv[T, w], hres[64 * w:64 * w + 64, T, :]).then_inc(s("acc_init"), 16)
            def bx_hi(b):
                act.wait_ge(s("bx_tr"), b + 1)
                nc.scalar.activation(xT[:, 0].rearrange("p c q -> p (c q)"), bank[7][:, 0:D], ACT.Copy,
                                     scale=XS).then_inc(s("bx_hi"), 1)

            g_act(0)
            for T in range(TILES):
                if T + 1 < TILES:
                    g_act(T + 1)
                g_hi(T)
                for c in LATE_CHUNKS[T]:
                    expert_hi(act, 6 + c // 6, c % 6)
                if T >= 2:
                    acc_init(T - 2)
            bx_hi(0)
            acc_init(TILES - 2)
            acc_init(TILES - 1)

            def silu(b):
                for i in range(2):
                    act.wait_ge(s(f"bg{i}"), b + 1)
                    nc.scalar.activation(gate[:, i * HALF:(i + 1) * HALF], bank[2 * i][:, 0:HALF], ACT.Silu,
                                         scale=1 / (XS * WS)).then_inc(s(f"ba{i}"), 1)

            def h_hi(b):
                act.wait_ge(s("bh_tr"), b + 1)
                nc.scalar.activation(hidT[:, 0, 0:4, :].rearrange("p c q -> p (c q)"), bank[4][:, :], ACT.Copy,
                                     scale=HS).then_inc(s("bh_hi"), 1)
                nc.scalar.activation(hidT[:, 0, 4, :], bank[5][:, 0:P], ACT.Copy, scale=HS)
                nc.scalar.activation(hidT[0:HLAST, 0, 5, :], bank[5][0:HLAST, P:2 * P], ACT.Copy,
                                     scale=HS).then_inc(s("bh_hi"), 1)
            with act.Fori(0, BLOCKS - 1) as b:
                silu(b)
                bx_hi(b + 1)
                h_hi(b)
            silu(BLOCKS - 1)
            h_hi(BLOCKS - 1)

        @block.vector
        def _(dve):
            v = nc.vector
            for i in range(3):
                dve.wait_ge(s("fw_hi"), i + 1)
                v.scalar_tensor_tensor(wprojT[:, 1, i * 512:(i + 1) * 512], bank[4 + i][:, :], WS,
                                       wprojT[:, 0, i * 512:(i + 1) * 512], ALU.mult, ALU.subtract).then_inc(s("fw_lo"), 1)

            def w_lo(m):
                dve.wait_ge(s("fw_hi"), m + 4)
                v.scalar_tensor_tensor(wT[:, 1, m], bank[7][:, :], WS, wT[:, 0, m], ALU.mult,
                                       ALU.subtract).then_inc(s("fw_lo"), 1)

            def px_lo(T, i):
                c0, c1 = ((0, 512), (512, PD))[i]
                b = bank[2 * (T % 2) + i]
                dve.wait_ge(s("px_hi"), 2 * T + i + 1)
                v.scalar_tensor_tensor(pxT[:, T % 2, 1, c0:c1], b[:, 0:c1 - c0], PS, pxT[:, T % 2, 0, c0:c1],
                                       ALU.mult, ALU.subtract).then_inc(s("px_lo"), 1)

            def ln_res(T, res, mm, psum, scale):
                dve.wait_ge(s(mm), T + 1)
                v.scalar_tensor_tensor(hres[:, T, :], psum, scale, hres[:, T, :], ALU.mult, ALU.add).then_inc(s(res), 1)

            def ln_stats(T, sfx, res):
                dve.wait_ge(s(res), T + 1)
                v.bn_stats(stats[:, T, :], hres[:, T, :]).then_inc(s("st" + sfx), 1)

            def ln_moments(T, sfx):
                dve.wait_ge(s("st" + sfx), T + 1)
                v.bn_aggr(mv[:, T, :], stats[:, T, :]).then_inc(s("ag" + sfx), 1)

            def ln_rstd(T, sfx):
                dve.wait_ge(s("sd" + sfx), T + 1)
                v.reciprocal(rstd[:, T:T + 1], std[:, T:T + 1]).then_inc(s("rs" + sfx), 1)

            def ln_apply(T, sfx, xh, dst):
                dve.wait_ge(s("rs" + sfx), T + 1)
                v.tensor_scalar(dst, hres[:, T, :], mv[:, T, 0:1], rstd[:, T:T + 1], ALU.subtract,
                                ALU.mult).then_inc(s(xh), 1)

            def x_lo(T, c):
                dve.wait_ge(s("x_hi"), T + 1)
                v.scalar_tensor_tensor(x1_at(1, c, T), bank[6][:, c * P:(c + 1) * P].rearrange("p (w j) -> p w j", w=2),
                                       XS, x1_at(0, c, T), ALU.mult, ALU.subtract).then_inc(s("x_lo"), 1)
            for T in range(2):
                for i in range(2):
                    px_lo(T, i)

            def patch_res(T):
                if T % 3 == 0:
                    dve.wait_ge(s("pb_add"), T // 3 + 1)
                ln_res(T, "h_res", "h_mm", bank[4 + T % 2][:, 0:D], 1 / (PS * WS))
            patch_res(0)
            ln_stats(0, "", "h_res")
            ln_moments(0, "")
            for T in range(TILES):
                ln_rstd(T, "")
                if T + 2 < TILES:
                    px_lo(T + 2, 0)
                ln_apply(T, "", "xh", xh1[:, T % 3, :])
                if T:
                    for c in range(DC):
                        x_lo(T - 1, c)
                if T < 4:
                    w_lo(T)
                if T + 1 < TILES:
                    patch_res(T + 1)
                if T + 2 < TILES:
                    px_lo(T + 2, 1)
                if T + 1 < TILES:
                    ln_stats(T + 1, "", "h_res")
                    ln_moments(T + 1, "")
            for c in range(DC):
                x_lo(TILES - 1, c)

            def qk_lo(g, a):
                dve.wait_ge(s("qk_hi"), g + 1)
                b = bank[0][:, 0:4 * GT].rearrange("p (m q) -> p m q", m=4)
                for m, scale in enumerate((even[:, :], odd[:, :], AS / (XS * WS))):
                    ins = v.scalar_tensor_tensor(qk[:, a, 1, 2 * m:2 * m + 2, :], b[:, 2 * (m // 2):2 * (m // 2) + 2, :],
                                                 scale, qk[:, a, 0, 2 * m:2 * m + 2, :], ALU.mult, ALU.subtract)
                ins.then_inc(s("qk_lo"), 1)

            def oT_lo(g, nj):
                dve.wait_ge(s("oT_hi"), g + 1)
                for c in range(DC):
                    at = [oT[:, h, c, :, bass.ds(6 * g, nj)] for h in range(2)]
                    ins = v.scalar_tensor_tensor(at[1], turned_o(c, nj), AS, at[0], ALU.mult, ALU.subtract)
                ins.then_inc(s("oT_lo"), 1)

            def masked(g, a):
                for r in range(4):
                    dve.wait_ge(s("sq"), 4 * g + r + 1)
                    pr = probs[0:GT, a, 4 * r:4 * r + 4, :]
                    v.scalar_tensor_tensor(pr, pr, 1.0, amask[0:GT, :].unsqueeze(1).to_broadcast([GT, 4, GT]),
                                           ALU.add, ALU.mult).then_inc(s("a_rdy"), 1)

            def o_norm(g, a):
                dve.wait_ge(s("o_turn"), g + 1)
                ov = bank[7][0:GT, :].rearrange("p (h d) -> p h d", h=HEADS)
                v.tensor_scalar(zz[0:GT, a, :], ov[:, :, HD], 2 * ATT_EPS, None, ALU.add).then_inc(s("o_z"), 1)
                dve.wait_ge(s("o_z"), g + 1)
                v.reciprocal(rz[0:GT, a, :], zz[0:GT, a, :]).then_inc(s("o_r"), 1)
                dve.wait_ge(s("o_r"), g + 1)
                v.tensor_tensor(onorm[0:GT, a, :].rearrange("p (h d) -> p h d", h=HEADS), ov[:, :, 0:HD],
                                rz[0:GT, a, :].unsqueeze(2).to_broadcast([GT, HEADS, HD]), ALU.mult).then_inc(s("o_n"), 1)
            def attend(g, a, e, chunks):
                start = g if isinstance(g, int) else 2
                for c in chunks[:1]:
                    expert_lo(dve, e, c)
                if start >= 2:
                    oT_lo(g - 2, 6)
                masked(g, a)
                if start >= 1:
                    o_norm(g - 1, 1 - a)
                for c in chunks[1:2]:
                    expert_lo(dve, e, c)
                if start < GROUPS - 1:
                    qk_lo(g + 1, 1 - a)
                for c in chunks[2:]:
                    expert_lo(dve, e, c)
            for c in range(2):
                expert_lo(dve, 0, c)
            dve.wait_ge(s("consts"), 1)
            qk_lo(0, 0)
            attend(0, 0, 0, range(2, 6))
            attend(1, 1, 1, range(0, 3))
            attend(2, 0, 1, range(3, 6))
            with dve.Fori(1, 4) as i:
                attend(2 * i + 1, 1, i + 1, range(0, 3))
                attend(2 * i + 2, 0, i + 1, range(3, 6))
            attend(9, 1, 5, range(0, 3))
            attend(10, 0, 5, range(3, 4))
            oT_lo(GROUPS - 2, 6)
            o_norm(GROUPS - 1, 0)
            oT_lo(GROUPS - 1, 64 - 6 * (GROUPS - 1))

            dve.wait_ge(s("zero_done"), 16 * (-(-BLOCKS // 3) + 1))
            dve.wait_ge(s("tok_i"), 1)
            v.tensor_scalar(tokid[64:P, :], tokid[64:P, :], 18 * 64 - 1, None, ALU.subtract).then_inc(s("tok_i"), 1)
            dve.wait_ge(s("tok_i"), 2)

            def x2_lo(T):
                dve.wait_ge(s("x2_hi"), T + 1)
                v.scalar_tensor_tensor(x2T[:, T, 1].rearrange("p c q -> p (c q)"), bank[2 + T % 2][:, 0:D], XS,
                                       x2T[:, T, 0].rearrange("p c q -> p (c q)"), ALU.mult,
                                       ALU.subtract).then_inc(s("x2_lo"), 1)
            def attended_res(T):
                ln_res(T, "op_res", "op_mm", bank[OP[T % 4]][:, 0:D], 1 / (AS * WS))
            attended_res(0)
            ln_stats(0, "2", "op_res")
            ln_moments(0, "2")
            for T in range(TILES):
                ln_rstd(T, "2")
                if T + 1 < TILES:
                    attended_res(T + 1)
                ln_apply(T, "2", "xh2_s", xh2[:, T, 0:D])
                if T + 1 < TILES:
                    ln_stats(T + 1, "2", "op_res")
                if T:
                    x2_lo(T - 1)
                if T + 1 < TILES:
                    ln_moments(T + 1, "2")
                if T < 2:
                    expert_lo(dve, 5, 4 + T)
                elif T % 2 == 0:
                    shared_lo(dve, T // 2 - 1)
            x2_lo(TILES - 1)

            n = [0]

            def step(ins):
                n[0] += 1
                ins.then_inc(s("rt"), 1)
                dve.wait_ge(s("rt"), n[0])

            def bc(col):
                return col.unsqueeze(2).to_broadcast([P, TILES, E])

            incl, ends = tsum[0], csum[1]

            def choose_experts():
                dve.wait_ge(s("lg_mm"), TILES)
                lg = bank[4][:, 0:TILES * E].rearrange("p (t e) -> p t e", e=E)
                step(v.tensor_reduce(lmax, lg, AX.X, ALU.max))
                step(v.tensor_tensor(ldiff, lg, bc(lmax), ALU.subtract))
                dve.wait_ge(s("ex_s"), 1)
                step(v.tensor_reduce(esum, ex, AX.X, ALU.add))
                step(v.reciprocal(rsum, esum))
                step(v.tensor_tensor(score, ex, bc(rsum), ALU.mult))
                step(v.tensor_reduce(w_1, score, AX.X, ALU.max))
                step(v.tensor_tensor(eq1, score, bc(w_1), ALU.is_equal))
                step(v.tensor_tensor(cand1, eq1, rank[:, :].unsqueeze(1).to_broadcast([P, TILES, E]), ALU.mult))
                step(v.tensor_reduce(best1, cand1, AX.X, ALU.max))
                step(v.tensor_tensor(sel1, cand1, bc(best1), ALU.is_equal))
                step(v.scalar_tensor_tensor(score2, sel1, -2.0, score, ALU.mult, ALU.add))
                step(v.tensor_reduce(w_2, score2, AX.X, ALU.max))
                step(v.tensor_tensor(eq2, score2, bc(w_2), ALU.is_equal))
                step(v.tensor_tensor(cand2, eq2, rank[:, :].unsqueeze(1).to_broadcast([P, TILES, E]), ALU.mult))
                step(v.tensor_reduce(best2, cand2, AX.X, ALU.max))
                step(v.tensor_tensor(sel2, cand2, bc(best2), ALU.is_equal))
                v.tensor_tensor(sel, sel1, sel2, ALU.add).then_inc(s("sel_s"), 1)

            def slot_weights():
                v.tensor_copy(xh2[:, :, ROW - 1].bitcast(I32), tokid[:, :])
                v.tensor_tensor(xh2[:, :, D:D + E], score, sel1, ALU.mult).then_inc(s("rt"), 1)
                n[0] += 1
                dve.wait_ge(s("rt"), n[0])
                step(v.tensor_tensor(ps1, score, sel2, ALU.mult))
                step(v.tensor_tensor(xh2[:, :, D:D + E], xh2[:, :, D:D + E], ps1, ALU.add))

            def count_tokens():
                v.memset(tsum[0][:, 0:8, :], 0.0)
                v.memset(tsum[1][:, 0:8, :], 0.0)
                v.memset(csum[0][:, 0:8], 0.0)
                v.memset(csum[1][:, 0:8], 0.0)
                dve.wait_ge(s("pre_mm"), 1)
                step(v.tensor_copy(tsum[0][:, 8:, :], bank[5][:, P:P + TILES * E].rearrange("p (t e) -> p t e", e=E)))
                for i, d in enumerate((1, 2, 4, 8)):
                    was, now = tsum[i % 2], tsum[1 - i % 2]
                    step(v.tensor_tensor(now[:, 8:, :], was[:, 8:, :], was[:, 8 - d:8 - d + TILES, :], ALU.add))
                step(v.tensor_tensor(cmp_n, incl[:, 7 + TILES, :].unsqueeze(2).to_broadcast([P, E, TILES]),
                                     thr[:, :].unsqueeze(1).to_broadcast([P, E, TILES]), ALU.is_gt))
                step(v.tensor_reduce(csum[0][:, 8:], cmp_n, AX.X, ALU.add))
                for i, d in enumerate((1, 2, 4)):
                    was, now = csum[i % 2], csum[1 - i % 2]
                    step(v.tensor_tensor(now[:, 8:], was[:, 8:], was[:, 8 - d:8 - d + E], ALU.add))

            def place_tokens():
                step(v.tensor_tensor(pos, bank[5][:, 0:TILES * E].rearrange("p (t e) -> p t e", e=E),
                                     incl[:, 7:7 + TILES, :], ALU.add))
                step(v.scalar_tensor_tensor(pos, ends[:, 7:7 + E].unsqueeze(1).to_broadcast([P, TILES, E]),
                                            float(P), pos, ALU.mult, ALU.add))
                v.tensor_tensor(ps1, pos, sel1, ALU.mult)
                step(v.tensor_tensor(ps2, pos, sel2, ALU.mult))
                v.tensor_reduce(slot1f, ps1, AX.X, ALU.add)
                step(v.tensor_reduce(slot2f, ps2, AX.X, ALU.add))
                v.tensor_copy(slot[:, 0, :], slot1f)
                v.tensor_copy(slot[:, 1, :], slot2f).then_inc(s("slot_s"), 1)

            def blocks_experts():
                step(v.tensor_tensor(cmp_b, ends[:, 8:].unsqueeze(1).to_broadcast([P, BLOCKS, E]),
                                     bidx[:, :].unsqueeze(2).to_broadcast([P, BLOCKS, E]), ALU.is_le))
                step(v.tensor_reduce(blkf, cmp_b, AX.X, ALU.add))
                v.tensor_scalar(blk[:, :], blkf, float(E - 1), None, ALU.min).then_inc(s("blk_s"), 1)
                step(v.tensor_scalar(rblk, blkf, float(E - 1), -1.0, ALU.min, ALU.mult))
                step(v.tensor_scalar(rblk, rblk, float(E), None, ALU.add))
                step(v.tensor_tensor(onehot, rank[:, :].unsqueeze(1).to_broadcast([P, BLOCKS, E]),
                                     rblk.unsqueeze(2).to_broadcast([P, BLOCKS, E]), ALU.is_equal))

            def g_mul(T):
                dve.wait_ge(s("g_act"), T + 1)
                if T:
                    dve.wait_ge(s("g_tr"), T)
                v.scalar_tensor_tensor(hid[:, 0:SHID], bank[2 * (T % 2) + 1][:, 0:SHID], 1 / (XS * WS), gate[:, 0:SHID],
                                       ALU.mult, ALU.mult).then_inc(s("g_mul"), 1)

            def g_lo(T):
                dve.wait_ge(s("g_hi"), T + 1)
                v.scalar_tensor_tensor(shid[:, 1].rearrange("p c q -> p (c q)"), bank[6][:, 0:SHID], HS,
                                       shid[:, 0].rearrange("p c q -> p (c q)"), ALU.mult,
                                       ALU.subtract).then_inc(s("g_lo"), 1)

            def y_add(T):
                dve.wait_ge(s("y_mm"), T + 1)
                v.scalar_tensor_tensor(hres[:, T, :], bank[4][:, 0:D], 1 / (HS * WS), hres[:, T, :],
                                       ALU.mult, ALU.add).then_inc(s("y_add"), 1)
            def bx_lo(b):
                dve.wait_ge(s("bx_hi"), b + 1)
                v.scalar_tensor_tensor(xT[:, 1].rearrange("p c q -> p (c q)"), bank[7][:, 0:D], XS,
                                       xT[:, 0].rearrange("p c q -> p (c q)"), ALU.mult,
                                       ALU.subtract).then_inc(s("bx_lo"), 1)

            def shared_tile(T):
                if T:
                    y_add(T - 1)
                g_lo(T)
                if T + 1 < TILES:
                    g_mul(T + 1)
                for c in LATE_CHUNKS[T]:
                    expert_lo(dve, 6 + c // 6, c % 6)
            choose_experts()
            g_mul(0)
            slot_weights()
            count_tokens()
            shared_tile(0)
            place_tokens()
            shared_tile(1)
            blocks_experts()
            for T in range(2, TILES):
                shared_tile(T)
            bx_lo(0)
            y_add(TILES - 1)

            def slot_scores():
                dve.wait_ge(s("meta_in"), 16)
                step(v.tensor_tensor(erow, meta[:, :, 0:E], onehot, ALU.mult))
                step(v.tensor_reduce(wts[:, :], erow, AX.X, ALU.add))

            def mul(b):
                for i in range(2):
                    dve.wait_ge(s(f"ba{i}"), b + 1)
                    ins = v.scalar_tensor_tensor(hid[:, i * HALF:(i + 1) * HALF], bank[2 * i + 1][:, 0:HALF],
                                                 1 / (XS * WS), gate[:, i * HALF:(i + 1) * HALF], ALU.mult, ALU.mult)
                ins.then_inc(s("bm"), 1)

            def y_ev(b, a, added):
                if added is not None:
                    dve.wait_ge(s("acc_add"), added)
                dve.wait_ge(s("by_mm"), b + 1)
                v.tensor_scalar(ysb[:, a, :], bank[6][:, 0:D], wts[:, bass.ds(b, 1)], 1 / (HS * WS),
                                ALU.mult, ALU.mult).then_inc(s("by_ev"), 1)

            def h_lo(b):
                dve.wait_ge(s("bh_hi"), 2 * b + 1)
                v.scalar_tensor_tensor(hidT[:, 1, 0:4, :].rearrange("p c q -> p (c q)"), bank[4][:, :], HS,
                                       hidT[:, 0, 0:4, :].rearrange("p c q -> p (c q)"), ALU.mult, ALU.subtract)
                dve.wait_ge(s("bh_hi"), 2 * b + 2)
                v.scalar_tensor_tensor(hidT[:, 1, 4, :], bank[5][:, 0:P], HS, hidT[:, 0, 4, :], ALU.mult, ALU.subtract)
                v.scalar_tensor_tensor(hidT[0:HLAST, 1, 5, :], bank[5][0:HLAST, P:2 * P], HS, hidT[0:HLAST, 0, 5, :],
                                       ALU.mult, ALU.subtract).then_inc(s("bh_lo"), 1)
            for b in range(3):
                mul(b)
                bx_lo(b + 1)
                if b == 0:
                    slot_scores()
                if b:
                    y_ev(b - 1, (b - 1) % 2, None)
                h_lo(b)
            with dve.Fori(0, (BLOCKS - 5) // 2) as i:
                for a in (0, 1):
                    b = 2 * i + a + 3
                    mul(b)
                    bx_lo(b + 1)
                    y_ev(b - 1, a, 16 * (2 * i + a) + 16)
                    h_lo(b)
            for b in range(BLOCKS - 2, BLOCKS):
                mul(b)
                if b + 1 < BLOCKS:
                    bx_lo(b + 1)
                y_ev(b - 1, (b - 1) % 2, 16 * (b - 2))
                h_lo(b)
            y_ev(BLOCKS - 1, 0, 16 * (BLOCKS - 2))

        @block.tensor
        def _(pe):
            t = nc.tensor
            def passes(psum, stat, hi, lo, first, last):
                t.matmul(psum, stat(0), lo, start=first, stop=False)
                t.matmul(psum, stat(0), hi, start=False, stop=False)
                return t.matmul(psum, stat(1), hi, start=False, stop=last)

            def tr(T):
                pe.wait_ge(s(f"px_in{T % 3}"), 32 * (T // 3) + 32)
                for k in range(PDC):
                    ins = t.transpose(bank[2 * (T % 2) + k // 4][:, (k % 4) * P:(k % 4 + 1) * P],
                                      px[:, T % 3, k * P:(k + 1) * P], ident[:, :])
                ins.then_inc(s("px_tr"), 1)

            def turn_wproj():
                pe.wait_ge(s("wproj_in"), 16)
                for c in range(DC):
                    for k in range(PDC):
                        ins = t.transpose(bank[4 + k // 2][:, (k % 2) * D + c * P:(k % 2) * D + (c + 1) * P],
                                          wproj_nat[:, c, k * P:(k + 1) * P], ident[:, :])
                ins.then_inc(s("w_tr"), 1)

            def turn_w(m):
                if m == 0:
                    pe.wait_ge(s("w_in"), 64)
                else:
                    pe.wait_ge(s("fw_lo"), 3 + m)
                for c in range(DC):
                    for k in range(DC):
                        ins = t.transpose(bank[7][:, k * D + c * P:k * D + (c + 1) * P],
                                          w_nat[:, m, c, k * P:(k + 1) * P], ident[:, :])
                ins.then_inc(s("w_tr"), 1)

            def turn_gate():
                pe.wait_ge(s("gate_in"), 16)
                pe.wait_ge(s("fw_lo"), 7)
                for k in range(DC):
                    ins = t.transpose(bank[7][:, k * E:(k + 1) * E], gnat[:, k * P:(k + 1) * P], ident[0:E, 0:E])
                ins.then_inc(s("w_tr"), 1)

            def mm(T):
                pe.wait_ge(s("px_lo"), 2 * T + 2)
                if T == 0:
                    pe.wait_ge(s("fw_lo"), 3)
                elif T >= 2:
                    pe.wait_ge(s("h_res"), T - 1)
                for k in range(PDC):
                    ins = passes(bank[4 + T % 2][:, 0:D], lambda h: pxT[:, T % 2, h, k * P:(k + 1) * P],
                                 wprojT[:, 0, k * D:(k + 1) * D], wprojT[:, 1, k * D:(k + 1) * D], k == 0, k == PDC - 1)
                ins.then_inc(s("h_mm"), 1)

            def xt(T):
                pe.wait_ge(s("xh"), T + 1)
                if T:
                    pe.wait_ge(s("x_lo"), DC * T)
                for k in range(DC):
                    ins = t.transpose(bank[6][:, k * P:(k + 1) * P], xh1[:, T % 3, k * P:(k + 1) * P], ident[:, :])
                ins.then_inc(s("x_tr"), 1)
            pe.wait_ge(s("ident_s"), 1)
            tr(0)
            turn_wproj()
            tr(1)
            for T in range(TILES):
                mm(T)
                if T + 2 < TILES:
                    tr(T + 2)
                if T:
                    xt(T - 1)
                if T < 4:
                    turn_w(T)
                elif T == 5:
                    turn_gate()
            xt(TILES - 1)
            pe.wait_ge(s("x_lo"), DC * TILES)
            pe.wait_ge(s("gateT_s"), 1)
            pe.wait_ge(s("pad_z"), 2)

            def project(g, a, first=False):
                x = [[x1T[:, h, k, bass.ds(g * GT, GT)] for k in range(DC)] for h in range(2)]
                for m in range(2):
                    for c in range(DC):
                        for k in range(DC):
                            at = k * D + c * P
                            ins = passes(bank[0][:, (2 * m + c) * GT:(2 * m + c + 1) * GT],
                                         lambda h: wT[:, h, m, at:at + P], x[0][k], x[1][k], k == 0, k == DC - 1)
                ins.then_inc(s("qk_mm"), 1)
                if not first:
                    pe.wait_ge(s("v_ev"), g)
                for k in range(DC):
                    ins = passes(bank[1][0:GT, 0:D], lambda h: x[h][k], wT[:, 0, 2, k * D:(k + 1) * D],
                                 wT[:, 1, 2, k * D:(k + 1) * D], k == 0, k == DC - 1)
                ins.then_inc(s("v_mm"), 1)

            def scores(g, a):
                pe.wait_ge(s("qk_lo"), g + 1)
                for pair in ((0, 1), (2, 3)):
                    for c in range(DC):
                        for key, query in ((0, 1), (0, 0), (1, 0)):
                            for r in pair:
                                rows = slice(32 * r, 32 * r + 32)
                                ins = t.matmul(bank[2 + r][0:GT, 2 * c * GT:2 * (c + 1) * GT],
                                               qk[rows, a, key, 4 + c, :], qk[rows, a, query, c:c + 3:2, :],
                                               start=(key, query) == (0, 1), stop=key == 1)
                                if c == DC - 1 and key == 1:
                                    ins.then_inc(s("s_mm"), 1)

            def values(g, a):
                if not (isinstance(g, int) and g == 0):
                    pe.wait_ge(s("o_raw"), g)
                pe.wait_ge(s("v_ev"), g + 1)
                for r in range(4):
                    pe.wait_ge(s("a_rdy"), 4 * g + r + 1)
                    for i in range(4):
                        h = 8 * (i // 2) + 2 * r + i % 2
                        n = 32 * (h % 4)
                        ins = t.matmul(bank[6][n:n + VW, h // 4 * GT:(h // 4 + 1) * GT], vaug[0:GT, a, h, :],
                                       probs[0:GT, a, 4 * r + i, :], start=True, stop=True)
                ins.then_inc(s("o_mm"), 1)

            def by_query(g, before):
                pe.wait_ge(s("o_raw"), g + 1)
                if before:
                    pe.wait_ge(s("oT_lo"), g)
                for i in range(4):
                    ins = t.transpose(bank[7][0:GT, i * P:(i + 1) * P], oraw[:, i, :], ident[:, :])
                ins.then_inc(s("o_turn"), 1)

            def turn_o(g, a):
                pe.wait_ge(s("o_n"), g + 1)
                for k in range(DC):
                    ins = t.transpose(bank[7][:, k * GT:(k + 1) * GT], onorm[0:GT, a, k * P:(k + 1) * P],
                                      ident[0:GT, 0:GT])
                ins.then_inc(s("oT_mm"), 1)

            def attend(g, a):
                start = g if isinstance(g, int) else 2
                scores(g, a)
                if start >= 1:
                    by_query(g - 1, start >= 2)
                if start < GROUPS - 1:
                    project(g + 1, 1 - a)
                values(g, a)
                if start >= 1:
                    turn_o(g - 1, 1 - a)
            project(0, 0, first=True)
            attend(0, 0)
            attend(1, 1)
            attend(2, 0)
            with pe.Fori(1, 4) as i:
                attend(2 * i + 1, 1)
                attend(2 * i + 2, 0)
            attend(9, 1)
            attend(10, 0)
            by_query(GROUPS - 1, True)
            turn_o(GROUPS - 1, 0)

            pe.wait_ge(s("oT_lo"), GROUPS)

            def oproj(T):
                if T >= 4:
                    pe.wait_ge(s("op_res"), T - 3)
                for k in range(DC):
                    ins = passes(bank[OP[T % 4]][:, 0:D], lambda h: oT[:, h, k, 2 * T:2 * T + 2, :].rearrange("p w j -> p (w j)"),
                                 wT[:, 0, 3, k * D:(k + 1) * D], wT[:, 1, 3, k * D:(k + 1) * D], k == 0, k == DC - 1)
                ins.then_inc(s("op_mm"), 1)

            def x2t(T):
                pe.wait_ge(s("xh2_s"), T + 1)
                for k in range(DC):
                    ins = t.transpose(bank[2 + T % 2][:, k * P:(k + 1) * P], xh2[:, T, k * P:(k + 1) * P], ident[:, :])
                ins.then_inc(s("x2_tr"), 1)

            def logits(T):
                pe.wait_ge(s("x2_f"), T + 1)
                for k in range(DC):
                    ins = t.matmul(bank[4][:, T * E:(T + 1) * E], x2f[:, T % 2, k, :], gateT[:, k, :],
                                   start=(k == 0), stop=(k == DC - 1))
                ins.then_inc(s("lg_mm"), 1)
            for T in range(4):
                oproj(T)
            for T in range(TILES):
                if T >= 2:
                    pe.wait_ge(s("x2_lo"), T - 1)
                x2t(T)
                if T + 4 < TILES:
                    oproj(T + 4)
                if T:
                    logits(T - 1)
            logits(TILES - 1)

            def s_up(T):
                if T >= 2:
                    pe.wait_ge(s("g_mul"), T - 1)
                for i in range(2):
                    for k in range(DC):
                        o = (i * DC + k) * SHID
                        ins = passes(bank[2 * (T % 2) + i][:, 0:SHID], lambda h: x2T[:, T, h, k, :],
                                     shared_w[:, 0, o:o + SHID], shared_w[:, 1, o:o + SHID], k == 0, k == DC - 1)
                ins.then_inc(s("g_mm"), 1)
            pe.wait_ge(s("w_lo"), 40)
            pe.wait_ge(s("x2_lo"), TILES)
            s_up(0)
            pe.wait_ge(s("consts"), 1)
            pe.wait_ge(s("sel_s"), 1)
            selr = sel.rearrange("p t e -> p (t e)")
            t.matmul(bank[5][:, 0:TILES * E], tri[:, :], selr, start=True, stop=True)
            t.matmul(bank[5][:, P:P + TILES * E], ones[:, :], selr, start=True, stop=True).then_inc(s("pre_mm"), 1)

            def s_turn(T):
                pe.wait_ge(s("g_mul"), T + 1)
                if T:
                    pe.wait_ge(s("g_lo"), T)
                for k in range(SHC):
                    ins = t.transpose(bank[6][:, k * P:(k + 1) * P], hid[:, k * P:(k + 1) * P], ident[:, :])
                ins.then_inc(s("g_tr"), 1)

            def s_down(T):
                pe.wait_ge(s("g_lo"), T + 1)
                if T:
                    pe.wait_ge(s("y_add"), T)
                for k in range(SHC):
                    o = 2 * DC * SHID + k * D
                    ins = passes(bank[4][:, 0:D], lambda h: shid[:, h, k, :], shared_w[:, 0, o:o + D],
                                 shared_w[:, 1, o:o + D], k == 0, k == SHC - 1)
                ins.then_inc(s("y_mm"), 1)
            def bx(b, a, count):
                pe.wait_ge(s(f"x_in{a}"), count)
                for k in range(DC):
                    ins = t.transpose(bank[7][:, k * P:(k + 1) * P], xblk[:, a, k * P:(k + 1) * P], ident[:, :])
                ins.then_inc(s("bx_tr"), 1)

            for T in range(TILES):
                if T + 1 < TILES:
                    s_up(T + 1)
                if T:
                    s_down(T - 1)
                s_turn(T)
            bx(0, 0, 16)
            s_down(TILES - 1)

            pe.wait_ge(s("y_add"), TILES)
            pe.wait_ge(s("blk_s"), 1)
            pe.wait_ge(s("w_lo"), 52)

            def expert_of(b):
                return pe.value_load(blk[0:1, bass.ds(b, 1)], min_val=0, max_val=E - 1)

            def up(b):
                e = expert_of(b)
                pe.wait_ge(s("bx_lo"), b + 1)
                for i in range(2):
                    for j, base in enumerate((W1, W3)):
                        for k in range(DC):
                            o = base + k * HID + i * HALF
                            ins = passes(bank[2 * i + j][:, 0:HALF], lambda h: xT[:, h, k, :],
                                         expert_at(e, 0, o, HALF), expert_at(e, 1, o, HALF), k == 0, k == DC - 1)
                    ins.then_inc(s(f"bg{i}"), 1)

            def bturn(b):
                pe.wait_ge(s("bm"), b + 1)
                for k in range(HC):
                    m = P if k < HC - 1 else HLAST
                    ins = t.transpose(bank[4 + k // 4][0:m, (k % 4) * P:(k % 4 + 1) * P], hid[:, k * P:k * P + m],
                                      ident[:, :])
                ins.then_inc(s("bh_tr"), 1)

            def down(b):
                e = expert_of(b)
                pe.wait_ge(s("bh_lo"), b + 1)
                for k in range(HC):
                    m = P if k < HC - 1 else HLAST
                    o = W2 + k * D
                    ins = passes(bank[6][:, 0:D], lambda h: hidT[0:m, h, k, :], expert_at(e, 0, o, D)[0:m],
                                 expert_at(e, 1, o, D)[0:m], k == 0, k == HC - 1)
                ins.then_inc(s("by_mm"), 1)
            up(0)
            bx(1, 1, 16)
            bturn(0)
            with pe.Fori(0, (BLOCKS - 3) // 2) as i:
                for a in (0, 1):
                    b = 2 * i + a + 1
                    up(b)
                    bx(b + 1, a, 16 * i + 32)
                    down(b - 1)
                    bturn(b)
            up(BLOCKS - 2)
            bx(BLOCKS - 1, 0, 16 * ((BLOCKS + 1) // 2))
            down(BLOCKS - 3)
            bturn(BLOCKS - 2)
            up(BLOCKS - 1)
            down(BLOCKS - 2)
            bturn(BLOCKS - 1)
            down(BLOCKS - 1)


_INS = ["x", "L0_tok_W_proj", "L0_tok_b_proj", "L0_tok_pos_emb", "L0_attn_Wq", "L0_attn_Wk", "L0_attn_Wv", "L0_attn_Wo",
        "L0_ffn_gate_w", "L0_ffn_w1", "L0_ffn_w2", "L0_ffn_w3", "L0_ffn_sw1", "L0_ffn_sw2", "L0_ffn_sw3"]


def kernel(**inputs):
    import numpy as np
    import concourse.bacc as bacc
    from concourse.bass_utils import run_bass_kernel_spmd

    nc = bacc.Bacc("TRN2", target_bir_lowering=False, num_devices=1)
    arrays, args = {}, []
    for name in _INS:
        a = np.ascontiguousarray(inputs[name])
        arrays[f"in_{name}"] = a
        args.append(nc.dram_tensor(f"in_{name}", a.shape, mybir.dt.from_np(a.dtype), kind="ExternalInput").ap())
    args.append(nc.dram_tensor("out_0", (IMAGES, SEQ, D), F32, kind="ExternalOutput").ap())
    vit_moe(nc, *args)
    r = run_bass_kernel_spmd(nc, [arrays], core_ids=[0])
    return r.results[0]["out_0"]
```
